# Optimizing a Trainium2 kernel written in Bass

```python
import numpy as np
import jax
import jax.numpy as jnp

def _softmax(x, axis=-1):
    return jax.nn.softmax(x, axis=axis)

def _gelu(x):
    return jax.nn.gelu(x, approximate=True)

def _silu(x):
    return jax.nn.silu(x)

def _sigmoid(x):
    return jax.nn.sigmoid(x)

def _layernorm(x, axis=-1, eps=1e-05):
    m = jnp.mean(x, axis=axis, keepdims=True)
    v = jnp.var(x, axis=axis, keepdims=True)
    return (x - m) / jnp.sqrt(v + eps)

def _scatter_add(tgt, idx, src, axis=0):
    return tgt.at[idx].add(src)

def _segment_sum(src, seg, n):
    return jax.ops.segment_sum(src, seg, n)
kernel_name = 'mk_flamingo_gated_d1_seqx_r4_dd8f09'

def setup_inputs(seed: int=0):
    np.random.seed(seed)
    _w = jnp.asarray

    def _rec_inputs():
        import jax
        import jax.numpy as jnp
        _rk = jax.random.key(seed)
        x = 7.22e-05 + 1 * jax.random.normal(jax.random.fold_in(_rk, 1), (8, 256, 256), jnp.float32)
        _lenS = 256 - jax.random.randint(jax.random.fold_in(_rk, 7), (8,), 0, max(1, 256 // 4) + 1, jnp.int32)
        _lenS2 = 120 - jax.random.randint(jax.random.fold_in(_rk, 8), (8,), 0, max(1, 120 // 4) + 1, jnp.int32)
        _ctx_1024P = jax.random.normal(jax.random.fold_in(_rk, 11), (8, 16, 256), jnp.float32)
        _ctx_1024c = jax.random.dirichlet(jax.random.fold_in(_rk, 511), 0.3 * jnp.ones((16,), jnp.float32), (8, 120))
        _ctx_1024t = jnp.einsum('bsk,bkd->bsd', _ctx_1024c, _ctx_1024P)
        _ctx_1024t = _ctx_1024t * jax.lax.rsqrt(jnp.mean(jnp.square(_ctx_1024t)) + 1e-12) * 0.953939
        ctx_1024 = 4.13588e-05 + 0.999923 * (_ctx_1024t + 0.3 * jax.random.normal(jax.random.fold_in(_rk, 611), (8, 120, 256), jnp.float32))
        _g = jax.random.normal(jax.random.fold_in(_rk, 9001), (2, 1), jnp.float32)
        _g = jnp.sign(_g) * jnp.maximum(jnp.abs(_g), 1.0) + (_g == 0) * 1.0
        g_xattn = _g[0]
        g_ffn = _g[1]
        return (x, ctx_1024, g_xattn, g_ffn)
    x, ctx_1024, g_xattn, g_ffn = _rec_inputs()

    def _L0_xattn_setup():
        import jax, jax.numpy as jnp
        import numpy as np
        Q_HEADS, KV_HEADS, DIMS = (16, 4, 256)
        HEAD_DIM = DIMS // Q_HEADS
        GROUPS = Q_HEADS // KV_HEADS
        ROPE_BASE = 10000.0

        def rope(x):
            s, d = (x.shape[-2], x.shape[-1])
            inv_freq = 1.0 / ROPE_BASE ** (jnp.arange(0, d, 2, dtype=jnp.float32) / d)
            ang = jnp.arange(s, dtype=jnp.float32)[:, None] * inv_freq[None, :]
            cos, sin = (jnp.cos(ang), jnp.sin(ang))
            x1, x2 = (x[..., 0::2], x[..., 1::2])
            out = jnp.stack([x1 * cos - x2 * sin, x1 * sin + x2 * cos], axis=-1)
            return out.reshape(x.shape).astype(x.dtype)
        key = jax.random.key(seed)
        k1, k2, k3, k4, k5, k6 = jax.random.split(key, 6)
        B, S, E = (4, 512, 256)
        q = jax.random.normal(k1, (B, S, E), dtype=jnp.float32)
        kv = jax.random.normal(k2, (B, S, E), dtype=jnp.float32)
        sc = 1.0 / np.sqrt(E)
        Wq = jax.random.normal(k3, (E, Q_HEADS, HEAD_DIM), dtype=jnp.float32) * sc
        Wk = jax.random.normal(k4, (E, KV_HEADS, HEAD_DIM), dtype=jnp.float32) * sc
        Wv = jax.random.normal(k5, (E, KV_HEADS, HEAD_DIM), dtype=jnp.float32) * sc
        Wo = jax.random.normal(k6, (HEAD_DIM, E), dtype=jnp.float32) / np.sqrt(HEAD_DIM)
        return {'q': q, 'kv': kv, 'Wq': Wq, 'Wk': Wk, 'Wv': Wv, 'Wo': Wo}
    _L0_xattn_all = _L0_xattn_setup()
    _L0_xattn_in = {k: v for k, v in _L0_xattn_all.items() if k in ('Wq', 'Wk', 'Wv', 'Wo')}
    del _L0_xattn_all

    def _L0_ffn_setup():
        import jax, jax.numpy as jnp
        import numpy as np
        TOP_K = 2
        key = jax.random.key(seed)
        k1, k2, k3, k4 = jax.random.split(key, 4)
        B, S, H, I, E = (2, 512, 256, 1024, 8)
        return {'hidden_states': jax.random.normal(k1, (B, S, H), jnp.float32), 'gate_w': jax.random.normal(k2, (E, H), jnp.float32) * 0.02, 'gate_up_proj': jax.random.normal(k3, (E, 2 * I, H), jnp.float32) * 0.02, 'down_proj': jax.random.normal(k4, (E, H, I), jnp.float32) * 0.02}
    _L0_ffn_all = _L0_ffn_setup()
    _L0_ffn_in = {k: v for k, v in _L0_ffn_all.items() if k in ('gate_w', 'gate_up_proj', 'down_proj')}
    del _L0_ffn_all
    return {'x': x, 'ctx_1024': ctx_1024, 'g_xattn': g_xattn, 'g_ffn': g_ffn, 'L0_xattn_Wq': _L0_xattn_in['Wq'], 'L0_xattn_Wk': _L0_xattn_in['Wk'], 'L0_xattn_Wv': _L0_xattn_in['Wv'], 'L0_xattn_Wo': _L0_xattn_in['Wo'], 'L0_ffn_gate_w': _L0_ffn_in['gate_w'], 'L0_ffn_gate_up_proj': _L0_ffn_in['gate_up_proj'], 'L0_ffn_down_proj': _L0_ffn_in['down_proj']}

def reference(x, ctx_1024, g_xattn, g_ffn, L0_xattn_Wq, L0_xattn_Wk, L0_xattn_Wv, L0_xattn_Wo, L0_ffn_gate_w, L0_ffn_gate_up_proj, L0_ffn_down_proj):
    import jax
    import jax.numpy as jnp

    def _L0_xattn_ref(q, kv, Wq, Wk, Wv, Wo):
        import jax, jax.numpy as jnp
        import numpy as np
        Q_HEADS, KV_HEADS, DIMS = (16, 4, 256)
        HEAD_DIM = DIMS // Q_HEADS
        GROUPS = Q_HEADS // KV_HEADS
        ROPE_BASE = 10000.0

        def rope(x):
            s, d = (x.shape[-2], x.shape[-1])
            inv_freq = 1.0 / ROPE_BASE ** (jnp.arange(0, d, 2, dtype=jnp.float32) / d)
            ang = jnp.arange(s, dtype=jnp.float32)[:, None] * inv_freq[None, :]
            cos, sin = (jnp.cos(ang), jnp.sin(ang))
            x1, x2 = (x[..., 0::2], x[..., 1::2])
            out = jnp.stack([x1 * cos - x2 * sin, x1 * sin + x2 * cos], axis=-1)
            return out.reshape(x.shape).astype(x.dtype)
        B, S, E = q.shape
        qh = jnp.einsum('bse,ehd->bshd', q, Wq)
        kh = jnp.einsum('bse,ehd->bshd', kv, Wk)
        vh = jnp.einsum('bse,ehd->bshd', kv, Wv)
        qh = qh.reshape(B, S, KV_HEADS, GROUPS, HEAD_DIM).transpose(0, 3, 2, 1, 4)
        kh = kh.transpose(0, 2, 1, 3)
        vh = vh.transpose(0, 2, 1, 3)
        qh = rope(qh)
        kh = rope(kh)
        scores = jnp.einsum('bghsd,bhad->bhsa', qh, kh)
        attn = jax.nn.softmax(scores / HEAD_DIM ** 0.5, axis=-1)
        out = jnp.einsum('bhsa,bhad->bhsd', attn, vh)
        out = out.mean(axis=1)
        return out @ Wo

    def _L0_ffn_ref(hidden_states, gate_w, gate_up_proj, down_proj):
        import jax, jax.numpy as jnp
        import numpy as np
        TOP_K = 2
        B, S, H = hidden_states.shape
        E = gate_w.shape[0]
        x = hidden_states.reshape(-1, H)
        T = x.shape[0]
        probs = jax.nn.softmax(x @ gate_w.T, axis=-1)
        w, idx = jax.lax.top_k(probs, TOP_K)
        w = w / jnp.sum(w, axis=-1, keepdims=True)
        combine = jnp.zeros((T, E), x.dtype).at[jnp.arange(T)[:, None], idx].add(w)

        def step(acc, inputs):
            gup, dn, ce = inputs
            g, u = jnp.split(x @ gup.T, 2, axis=-1)
            acc = acc + ce[:, None] * (jax.nn.silu(g) * u @ dn.T)
            return (acc, None)
        out, _ = jax.lax.scan(step, jnp.zeros_like(x), (gate_up_proj, down_proj, combine.T))
        return out.reshape(B, S, H)
    x = x + jnp.tanh(g_xattn[0]) * _L0_xattn_ref(_layernorm(x, axis=-1), ctx_1024, L0_xattn_Wq, L0_xattn_Wk, L0_xattn_Wv, L0_xattn_Wo)
    x = x + jnp.tanh(g_ffn[0]) * _L0_ffn_ref(_layernorm(x, axis=-1), L0_ffn_gate_w, L0_ffn_gate_up_proj, L0_ffn_down_proj)
    return x

_drawn_inputs = setup_inputs


def setup_inputs(seed=0):
    import zlib

    import numpy as np

    out = dict(_drawn_inputs(seed))
    spreads = {}
    factors = {'L0_ffn_gate_w': 8.211}
    for name, (base, spread) in spreads.items():
        noise = np.random.default_rng([zlib.crc32(name.encode()), seed]).standard_normal(out[name].shape)
        drawn = base * np.exp(spread * noise) if base else spread * noise
        out[name] = jnp.asarray(drawn.astype(out[name].dtype))
    for name, factor in factors.items():
        out[name] = (out[name] * factor).astype(out[name].dtype)
    return out
```

```python
from contextlib import ExitStack

import numpy as np
import concourse.bass as bass
from concourse import mybir

F32 = mybir.dt.float32
F32R = mybir.dt.float32r
BF16 = mybir.dt.bfloat16
I32 = mybir.dt.int32
ALU = mybir.AluOpType
ACT = mybir.ActivationFunctionType
AX = mybir.AxisListType

P = 128
B, S, D = 8, 256, 256
A = 120
KVH, GROUPS, HD = 4, 4, 16
E, I = 8, 1024
T = B * S
NT = T // P
TB = S // P
KC = D // P
HR = 2 * HD
EPS = 1e-5
NBLK = (2 * T + E * (P - 1)) // P
NCOL = NBLK + 1
HALF = I // 2
JH = HALF // P
GU = KC * 2 * I
DN = (I // P) * D
RING = 4
MAGIC = float(0x5F3759DF)

CONSTS = {}


def _const_columns():
    at = 0
    for name, n in (("ident", P), ("rope", S), ("kcos", A), ("ksin", A), ("headmask", KVH * A),
                    ("before", P), ("iota", P), ("prio", E), ("steps", 15), ("upto", E * E),
                    ("blocks", NCOL), ("token1", NT), ("spare", 1)):
        CONSTS[name] = (at, at + n)
        at += n
    return at


NCONST = _const_columns()
WSMALL = {"wq": (0, 1024), "wka": (1024, 1280), "wkb": (1280, 1536), "wv": (1536, 1664),
          "gate": (1664, 1680), "tanh_in": (1680, 1682)}
NSMALL = 1682


def build_program(nc, x_d, ctx_d, small_d, wo_d, gu_d, dn_d, const_d, out_d):
    xn2_d = nc.dram_tensor("xn2_scratch", (T + P, D), F32, kind="Internal").ap()
    ctx = ExitStack()
    with ctx:
        def sb(name, shape, dt=F32):
            return ctx.enter_context(nc.sbuf_tensor(name, shape, dt))

        def sem(name):
            return ctx.enter_context(nc.semaphore(name))

        x = sb("x", [P, NT, D])
        const = sb("const", [P, NCONST])
        small = sb("small", [P, NSMALL])
        wo = sb("wo", [HD, D])
        area = sb("area", [P, 2 * NT * 3 * NCOL + 8 * P])
        ctxT = area[:, 0:KC * B * A].rearrange("p (k n) -> p k n", k=KC)
        krot = area[:, 1920:1920 + B * A].rearrange("p (b a) -> p b a", b=B)
        kbd = area[:, 2880:2880 + 2 * KVH * A].rearrange("p (q h a) -> p q h a", q=2, h=KVH)
        n0 = 4 * NT * NCOL
        spread = area[:, 0:n0].rearrange("p (n q s) -> p n q s", n=2 * NT, q=2)
        rcmp = area[:, n0:n0 + 2 * NT * NCOL]
        onehot = area[:, n0 + 2 * NT * NCOL:n0 + 2 * NT * NCOL + 8 * P].rearrange("p (n q) -> p n q", n=8)
        wq = sb("wq", [P, KC, P])
        v = sb("v", [A, B * KVH * HD])
        stats = sb("stats", [P, NT, 6])
        mv = sb("mv", [P, NT, 2])
        mv2 = sb("mv2", [P, NT, 2])
        rstd = sb("rstd", [P, NT])
        rstd2 = sb("rstd2", [P, NT])
        nwt = sb("nwt", [P, 3, NT])
        xn = sb("xn", [P, 2, TB, D])
        xnT = sb("xnT", [P, KC, S])
        qrot = sb("qrot", [P, S])
        probs = sb("probs", [P, TB, KVH, A])
        ktmp = probs[:, 0, :, :]
        negmax = sb("negmax", [P, TB, KVH])
        den = sb("den", [P, TB, KVH])
        probsT = area[0:A, 3840:3840 + KVH * S].rearrange("a (h s) -> a h s", h=KVH)
        oT = sb("oT", [HD, S])
        xn2 = sb("xn2", [P, TB, D])
        xn2T = sb("xn2T", [P, KC, S])
        tg = sb("tg", [P, 2])
        zrow = sb("zrow", [P, D])
        logits = sb("logits", [P, NT, E])
        ra, rb, rexp = (small[:, n * NT * E:(n + 1) * NT * E].rearrange("p (t e) -> p t e", e=E) for n in range(3))
        pick = small[:, 3 * NT * E:5 * NT * E].rearrange("p (k t e) -> p k t e", k=2, e=E)
        pmax = sb("pmax", [P, 2, NT])
        pscore = sb("pscore", [P, NT])
        chosen = sb("chosen", [P, NT + 1, E], BF16)
        before_bf = sb("before_bf", [P, P], BF16)
        ones_bf = sb("ones_bf", [P, P], BF16)
        slotpos = sb("slotpos", [P, NT + 1, E])
        nblk = sb("nblk", [P, E])
        endblk = sb("endblk", [P, E])
        startslot = sb("startslot", [P, E])
        slot = sb("slot", [P, 2, NT])
        slot_i = sb("slot_i", [P, 2, 2 * NT], I32)
        slot_f = sb("slot_f", [P, 2, 2 * NT])
        wslot = sb("wslot", [P, NCOL])
        idxf = sb("idxf", [P, 2, NCOL])
        idx = sb("idx", [P, NCOL], I32)
        tabf = sb("tabf", [P, 3, NCOL])
        tab = sb("tab", [P, 2, NCOL], I32)
        idx_g = sb("idx_g", [P, 1], I32)
        idx_s = sb("idx_s", [P, 1], I32)
        wraw = sb("wraw", [P, GU + DN])
        gu = sb("gu", [P, 2, 2, GU], F32R)
        dn = sb("dn", [P, 2, 2, DN], F32R)
        late = x[:, :, :].rearrange("p t d -> p (t d)")
        xg = late[:, 0:RING * D].rearrange("p (r d) -> p r d", r=RING)
        y = late[:, RING * D:2 * RING * D].rearrange("p (r d) -> p r d", r=RING)
        silu = late[:, 2 * RING * D:2 * RING * D + I].rearrange("p (q n) -> p q n", q=2)
        h = late[:, 2 * RING * D + I:2 * RING * D + 2 * I].rearrange("p (q n) -> p q n", q=2)
        xs = xn[:, 0, 0, :]
        xT = sb("xT", [P, 2, 2, KC, P], F32R)
        hT = sb("hT", [P, 2, 2, JH * P], F32R)
        bank = [ctx.enter_context(nc.psum_tensor(f"bank{i}", [P, 512], F32)) for i in range(8)]

        def c(name, n=P):
            a, b = CONSTS[name]
            return const[0:n, a:b]

        ident = c("ident")

        const_in, small_in, wo_in, ctx_in = (sem(n) for n in ("const_in", "small_in", "wo_in", "ctx_in"))
        x_in = [sem(f"x_in{b}") for b in range(B)]
        dve_step, act_step, pool_step = sem("dve_step"), sem("act_step"), sem("pool_step")
        wq_summed, k_psum, krot_ready, kbd_ready, v_psum, v_ready, tanh_ready = (
            sem(n) for n in ("wq_summed", "k_psum", "krot_ready", "kbd_ready", "v_psum", "v_ready", "tanh_ready"))
        xn_ready, xnT_psum, xnT_ready, q_psum, qrot_ready, s_psum, negmax_ready, exp_done, probs_ready = (
            sem(n) for n in ("xn_ready", "xnT_psum", "xnT_ready", "q_psum", "qrot_ready", "s_psum",
                             "negmax_ready", "exp_done", "probs_ready"))
        pT_psum, pT_act, pT_dve, o_psum, oT_ready, att_psum, x2_ready = (
            sem(n) for n in ("pT_psum", "pT_act", "pT_dve", "o_psum", "oT_ready", "att_psum", "x2_ready"))
        xn2_ready, xn2T_psum, xn2T_ready, lg_psum, lg_ready = (
            sem(n) for n in ("xn2_ready", "xn2T_psum", "xn2T_ready", "lg_psum", "lg_ready"))
        out_init, xn2_out, zrow_ready, zero_xn2, zero_out = (
            sem(n) for n in ("out_init", "xn2_out", "zrow_ready", "zero_xn2", "zero_out"))
        shifted, rexp_ready, chosen_ready, rank_psum, onehot_ready, onehot_used, slots_psum, tables_ready = (
            sem(n) for n in ("shifted", "rexp_ready", "chosen_ready", "rank_psum", "onehot_ready", "onehot_used",
                             "slots_psum", "tables_ready"))
        gu_in, dn_in, w_split = sem("gu_in"), sem("dn_in"), sem("w_split")
        index_settled = sem("index_settled")
        idx_g_ready, idx_s_ready, x_gathered, y_added, y_free = (
            sem(n) for n in ("idx_g_ready", "idx_s_ready", "x_gathered", "y_added", "y_free"))
        x_staged, xT_made, xT_hi, xT_split = (sem(n) for n in ("x_staged", "xT_made", "xT_hi", "xT_split"))
        gu_made, silu_made, h_made, hT_made, hT_hi, hT_split, y_made, y_out = (
            sem(n) for n in ("gu_made", "silu_made", "h_made", "hT_made", "hT_hi", "hT_split", "y_made", "y_out"))

        block = ctx.enter_context(nc.Block())
        SPLITS = 6

        @block.sync
        def _(sp):
            sp.dma_start(small[:, :], small_d).then_inc(small_in, 16)
            sp.dma_start(ctxT[:, :, :], ctx_d).then_inc(ctx_in, 16)
            sp.dma_start(const[:, :], const_d).then_inc(const_in, 16)
            x_v = x_d.rearrange("(t p) d -> p t d", p=P)
            for b in range(B):
                sp.dma_start(x[:, TB * b:TB * b + TB, :], x_v[:, TB * b:TB * b + TB, :]).then_inc(x_in[b], 16)
            sp.dma_start(wo[:, :], wo_d).then_inc(wo_in, 16)

            def load_expert(e):
                if e >= 1:
                    sp.wait_ge(w_split, SPLITS * e)
                sp.dma_start(wraw[:, 0:GU], gu_d[e]).then_inc(gu_in, 16)
                sp.dma_start(wraw[:, GU:GU + DN], dn_d[e]).then_inc(dn_in, 16)

            load_expert(0)
            sp.wait_ge(zrow_ready, 1)
            sp.dma_start(out_d[T:T + P, :], zrow[:, :]).then_inc(zero_out, 16)
            sp.dma_start(xn2_d[T:T + P, :], zrow[:, :]).then_inc(zero_xn2, 16)
            out_v = out_d[0:T, :].rearrange("(t p) d -> p t d", p=P)
            xn2_v = xn2_d[0:T, :].rearrange("(t p) d -> p t d", p=P)
            for b in range(B):
                sp.wait_ge(x2_ready, TB * (b + 1))
                sp.dma_start(out_v[:, TB * b:TB * b + TB, :], x[:, TB * b:TB * b + TB, :]).then_inc(out_init, 16)
                sp.wait_ge(xn2_ready, TB * (b + 1))
                sp.dma_start(xn2_v[:, TB * b:TB * b + TB, :], xn2[:, :, :]).then_inc(xn2_out, 16)
                if b == 3:
                    load_expert(1)
            for e in range(2, E):
                load_expert(e)
            sp.wait_ge(out_init, 16 * B)
            sp.wait_ge(zero_out, 16)
            sp.wait_ge(y_added, 16 * NBLK)

        @block.gpsimd
        def _(pool):
            nc.gpsimd.memset(zrow[:, :], 0.0).then_inc(zrow_ready, 1)
            nc.gpsimd.memset(ones_bf[:, :], 1.0).then_inc(pool_step, 1)
            pool.sem_inc(y_free, RING)

            def split(raw, hi, lo, n_done):
                nc.gpsimd.tensor_tensor(hi, raw, zrow[:, 0:1].broadcast_to([P, raw.shape[1]]), ALU.add).then_inc(w_split, 1)
                pool.wait_ge(w_split, n_done + 1)
                nc.gpsimd.tensor_tensor(lo, raw, hi, ALU.subtract).then_inc(w_split, 1)

            def split_expert(where, n_done, part=None):
                half = GU // 2
                for k in range(3) if part is None else (part,):
                    if k < 2:
                        hi = gu[:, :, :, :].rearrange("p s q n -> p (s q n)")
                        split(wraw[:, k * half:(k + 1) * half],
                              hi[:, bass.ds(where * (2 * GU) + k * half, half)],
                              hi[:, bass.ds(where * (2 * GU) + GU + k * half, half)], n_done + 2 * k)
                    else:
                        hi = dn[:, :, :, :].rearrange("p s q n -> p (s q n)")
                        split(wraw[:, GU:GU + DN], hi[:, bass.ds(where * (2 * DN), DN)],
                              hi[:, bass.ds(where * (2 * DN) + DN, DN)], n_done + 2 * k)

            def spread_keys(b):
                pool.wait_ge(krot_ready, 2)
                if b >= 2:
                    pool.wait_ge(s_psum, TB * (b - 1))
                mask = c("headmask").rearrange("p (h a) -> p h a", h=KVH)
                nc.gpsimd.tensor_tensor(kbd[:, b % 2, :, :],
                                        krot[:, b, :].rearrange("p (o a) -> p o a", o=1).broadcast_to([P, KVH, A]),
                                        mask, ALU.mult).then_inc(kbd_ready, 1)

            pool.wait_ge(const_in, 16)
            pool.wait_ge(zrow_ready, 1)
            spread_keys(0)
            spread_keys(1)
            for b in range(B):
                if b + 2 < B:
                    spread_keys(b + 2)
                if b == 0:
                    pool.wait_ge(gu_in, 16)
                    pool.wait_ge(dn_in, 16)
                if b == 4:
                    pool.wait_ge(gu_in, 32)
                    pool.wait_ge(dn_in, 32)
                if b in (0, 1, 2):
                    split_expert(0, 0, b)
                if b in (4, 5, 6):
                    split_expert(1, SPLITS, b - 4)

            def gather(g, r):
                nc.gpsimd.tensor_copy(idx_g[:, :], idx[:, bass.ds(g, 1)]).then_inc(idx_g_ready, 1)
                pool.wait_ge(idx_g_ready, g + 1)
                pool.sem_inc(index_settled, 1)
                nc.gpsimd.indirect_dma_start(
                    out=xg[:, r, :], out_offset=None, in_=xn2_d,
                    in_offset=bass.IndirectOffsetOnAxis(ap=idx_g[:, :], axis=0)).then_inc(x_gathered, 16)

            def scatter(n, r):
                pool.wait_ge(y_out, n + 1)
                nc.gpsimd.tensor_copy(idx_s[:, :], idx[:, bass.ds(n, 1)]).then_inc(idx_s_ready, 1)
                pool.wait_ge(idx_s_ready, n + 1)
                pool.sem_inc(index_settled, 1)
                nc.gpsimd.indirect_dma_start(
                    out=out_d, out_offset=bass.IndirectOffsetOnAxis(ap=idx_s[:, :], axis=0),
                    in_=y[:, r, :], in_offset=None, compute_op=ALU.add).then_inc(y_added, 16)

            def next_expert(s):
                e = pool.value_load(tab[0:1, 1, bass.ds(s, 1)], min_val=0, max_val=E - 2)
                with pool.If(e > 0):
                    pool.wait_ge(gu_in, 16 * (e + 2))
                    pool.wait_ge(dn_in, 16 * (e + 2))
                    pool.wait_ge(y_made, s)
                    split_expert((e + 1) & 1, SPLITS * (e + 1))

            def step(s, r, ahead=True):
                scatter(s - 1, r)
                if ahead:
                    pool.wait_ge(x_gathered, 16 * (s + 3))
                    pool.wait_ge(x_staged, s)
                    gather(s + 3, r)
                pool.wait_ge(y_added, 16 * s)
                pool.sem_inc(y_free, 1)
                next_expert(s)

            pool.wait_ge(tables_ready, 1)
            pool.wait_ge(xn2_out, 16 * B)
            pool.wait_ge(zero_xn2, 16)
            pool.wait_ge(zero_out, 16)
            pool.wait_ge(out_init, 16 * B)
            for g in range(RING):
                if g >= 1:
                    pool.wait_ge(x_gathered, 16 * g)
                gather(g, g)
            LOOPED = (NBLK - 1 - 2) // RING
            with pool.Fori(0, LOOPED) as i:
                for u in range(RING):
                    step(i * RING + (u + 1), u)
            for s in range(LOOPED * RING + 1, NBLK):
                step(s, (s - 1) % RING, ahead=False)
            scatter(NBLK - 1, (NBLK - 1) % RING)

        @block.scalar
        def _(act):
            act.wait_ge(small_in, 16)
            a0, a1 = WSMALL["tanh_in"]
            nc.scalar.activation(tg[:, :], small[:, a0:a1], ACT.Tanh).then_inc(tanh_ready, 1)
            act.wait_ge(v_psum, 1)
            nc.scalar.activation(v[:, :], bank[7][0:A, :], ACT.Copy).then_inc(v_ready, 1)
            for t in range(B + 2):
                if t < B:
                    act.wait_ge(xnT_psum, t + 1)
                    if t >= 1:
                        act.wait_ge(q_psum, t)
                    nc.scalar.activation(xnT[:, :, :].rearrange("p c s -> p (c s)"), bank[0][:, :],
                                         ACT.Copy).then_inc(xnT_ready, 1)
                if 1 <= t <= B:
                    b = t - 1
                    act.wait_ge(pT_psum, 2 * b + 1)
                    if b >= 1:
                        act.wait_ge(o_psum, b)
                    nc.scalar.activation(probsT[:, 0:2, :].rearrange("a h s -> a (h s)"), bank[4][0:A, :],
                                         ACT.Copy).then_inc(pT_act, 1)
                if t >= 2:
                    b = t - 2
                    act.wait_ge(xn2T_psum, b + 1)
                    if b >= 1:
                        act.wait_ge(lg_psum, b)
                    nc.scalar.activation(xn2T[:, :, :].rearrange("p c s -> p (c s)"), bank[0][:, :],
                                         ACT.Copy).then_inc(xn2T_ready, 1)
                if 1 <= t <= B:
                    b = t - 1
                    act.wait_ge(o_psum, b + 1)
                    if b >= 1:
                        act.wait_ge(att_psum, b)
                    nc.scalar.activation(oT[:, :], bank[6][0:HD, 0:S], ACT.Copy).then_inc(oT_ready, 1)
                if t < B:
                    for j in range(TB):
                        act.wait_ge(negmax_ready, TB * t + j + 1)
                        if t >= 1:
                            act.wait_ge(pT_psum, 2 * t)
                        for hh in range(KVH):
                            nc.scalar.activation(probs[:, j, hh, :], bank[2 + j][:, hh * A:(hh + 1) * A], ACT.Exp,
                                                 bias=negmax[:, j, hh:hh + 1], scale=HD ** -0.5,
                                                 accum_out=den[:, j, hh:hh + 1]).then_inc(exp_done, 1)
            act.wait_ge(shifted, 1)
            nc.scalar.activation(rexp[:, :, :], rb[:, :, :], ACT.Exp).then_inc(rexp_ready, 1)

            def stage(s):
                act.wait_ge(x_gathered, 16 * (s + 1))
                nc.scalar.activation(xs[:, :], xg[:, :, :].rearrange("p r d -> p (r d)")[:, bass.ds((s & (RING - 1)) * D, D)],
                                     ACT.Copy).then_inc(x_staged, 1)

            def x_high(s, par):
                act.wait_ge(xT_made, s + 1)
                nc.scalar.activation(xT[:, par, 0, :, :].rearrange("p c t -> p (c t)"), bank[7][:, 0:D],
                                     ACT.Copy).then_inc(xT_hi, 1)

            def gate(s, hf):
                act.wait_ge(gu_made, 2 * s + hf + 1)
                if not isinstance(s, int) or s >= 1:
                    act.wait_ge(h_made, 2 * s + hf - 1)
                nc.scalar.activation(silu[:, hf, :], bank[2 * hf][:, :], ACT.Silu).then_inc(silu_made, 1)

            def h_high(s, hf):
                act.wait_ge(hT_made, 2 * s + hf + 1)
                nc.scalar.activation(hT[:, hf, 0, :], bank[4 + hf][:, :], ACT.Copy).then_inc(hT_hi, 1)

            def step(s, par, first=False, ahead=2):
                gate(s, 0)
                if not first:
                    h_high(s - 1, 1)
                if ahead >= 1:
                    x_high(s + 1, 1 - par)
                if ahead >= 2:
                    stage(s + 2)
                gate(s, 1)
                h_high(s, 0)

            stage(0)
            x_high(0, 0)
            stage(1)
            step(0, 0, first=True)
            with act.Fori(0, (NBLK - 3) // 2) as i:
                step(i * 2 + 1, 1)
                step(i * 2 + 2, 0)
            step(NBLK - 2, 1, ahead=1)
            step(NBLK - 1, 0, ahead=0)
            h_high(NBLK - 1, 1)

        @block.tensor
        def _(pe):
            wka = small[:, 1024:1280].rearrange("p (c n) -> p c n", c=KC)
            wkb = small[:, 1280:1536].rearrange("p (c n) -> p c n", c=KC)
            wv = small[:, 1536:1664].rearrange("p (c n) -> p c n", c=KC)
            gw = small[:, 1664:1680].rearrange("p (c n) -> p c n", c=KC)
            pe.wait_ge(small_in, 16)
            pe.wait_ge(ctx_in, 16)
            for g in range(2):
                for n, w in enumerate((wka, wkb)):
                    for k in range(KC):
                        mm = nc.tensor.matmul(bank[2 + 2 * g + n][:, 0:4 * A], w[:, k, :],
                                              ctxT[:, k, 4 * A * g:4 * A * (g + 1)], start=(k == 0), stop=(k == KC - 1))
                mm.then_inc(k_psum, 1)
            for b in range(B):
                for k in range(KC):
                    mm = nc.tensor.matmul(bank[7][0:A, b * 64:(b + 1) * 64], ctxT[:, k, b * A:(b + 1) * A],
                                          wv[:, k, :], start=(k == 0), stop=(k == KC - 1))
            mm.then_inc(v_psum, 1)
            pe.wait_ge(const_in, 16)
            pe.wait_ge(wq_summed, 1)
            for t in range(B + 2):
                if t < B:
                    pe.wait_ge(xn_ready, TB * (t + 1))
                    if t >= 3:
                        pe.wait_ge(xn2T_ready, t - 2)
                    for j in range(TB):
                        for k in range(KC):
                            mm = nc.tensor.transpose(bank[0][:, k * S + j * P:k * S + (j + 1) * P],
                                                     xn[:, t % 2, j, k * P:(k + 1) * P], ident)
                    mm.then_inc(xnT_psum, 1)
                if 1 <= t <= B:
                    b = t - 1
                    pe.wait_ge(probs_ready, TB * (b + 1))
                    if b == 0:
                        pe.wait_ge(krot_ready, 2)
                    else:
                        pe.wait_ge(pT_act, b)
                        pe.wait_ge(pT_dve, b)
                    for g in range(2):
                        for hh in range(2):
                            for j in range(TB):
                                mm = nc.tensor.transpose(bank[4 + g][0:A, hh * S + j * P:hh * S + (j + 1) * P],
                                                         probs[:, j, 2 * g + hh, :], ident)
                        mm.then_inc(pT_psum, 1)
                if t < B:
                    pe.wait_ge(xnT_ready, t + 1)
                    if t >= 1:
                        pe.wait_ge(qrot_ready, t)
                    for k in range(KC):
                        mm = nc.tensor.matmul(bank[1][:, 0:S], wq[:, k, :], xnT[:, k, :],
                                              start=(k == 0), stop=(k == KC - 1))
                    mm.then_inc(q_psum, 1)
                if t >= 2:
                    b = t - 2
                    pe.wait_ge(xn2_ready, TB * (b + 1))
                    if t >= B and b >= 1:
                        pe.wait_ge(xn2T_ready, b)
                    for j in range(TB):
                        for k in range(KC):
                            mm = nc.tensor.transpose(bank[0][:, k * S + j * P:k * S + (j + 1) * P],
                                                     xn2[:, j, k * P:(k + 1) * P], ident)
                    mm.then_inc(xn2T_psum, 1)
                if 1 <= t <= B:
                    b = t - 1
                    pe.wait_ge(pT_act, b + 1)
                    pe.wait_ge(pT_dve, b + 1)
                    pe.wait_ge(v_ready, 1)
                    if b >= 2:
                        pe.wait_ge(lg_ready, b - 1)
                    for hh in range(KVH):
                        mm = nc.tensor.matmul(bank[6][0:HD, 0:S], v[:, b * 64 + hh * HD:b * 64 + (hh + 1) * HD],
                                              probsT[:, hh, :], start=(hh == 0), stop=(hh == KVH - 1))
                    mm.then_inc(o_psum, 1)
                if t < B:
                    pe.wait_ge(qrot_ready, t + 1)
                    pe.wait_ge(kbd_ready, t + 1)
                    if t >= 1:
                        pe.wait_ge(exp_done, TB * KVH * t)
                    for j in range(TB):
                        nc.tensor.matmul(bank[2 + j][:, 0:KVH * A], qrot[:, j * P:(j + 1) * P],
                                         kbd[:, t % 2, :, :].rearrange("p h a -> p (h a)"),
                                         start=True, stop=True).then_inc(s_psum, 1)
                if 1 <= t <= B:
                    b = t - 1
                    pe.wait_ge(oT_ready, b + 1)
                    if b == 0:
                        pe.wait_ge(wo_in, 16)
                    else:
                        pe.wait_ge(x2_ready, TB * b)
                    for j in range(TB):
                        mm = nc.tensor.matmul(bank[7][:, j * D:(j + 1) * D], oT[:, j * P:(j + 1) * P], wo[:, :],
                                              start=True, stop=True)
                    mm.then_inc(att_psum, 1)
                if t >= 2:
                    b = t - 2
                    pe.wait_ge(xn2T_ready, b + 1)
                    pe.wait_ge(oT_ready, min(b + 2, B))
                    if b >= 1:
                        pe.wait_ge(lg_ready, b)
                    for j in range(TB):
                        for k in range(KC):
                            mm = nc.tensor.matmul(bank[6][:, S + j * E:S + (j + 1) * E],
                                                  xn2T[:, k, j * P:(j + 1) * P], gw[:, k, :],
                                                  start=(k == 0), stop=(k == KC - 1))
                    mm.then_inc(lg_psum, 1)

            pe.wait_ge(chosen_ready, 4)
            pe.wait_ge(pool_step, 1)
            flat = chosen[:, :, :].rearrange("p t e -> p (t e)")
            nc.tensor.matmul(bank[0][:, 0:(NT + 1) * E], before_bf[:, :], flat, start=True, stop=False)
            for t in range(NT):
                n = NT - t
                mm = nc.tensor.matmul(bank[0][:, (t + 1) * E:(NT + 1) * E], ones_bf[:, :],
                                      chosen[:, t:t + 1, :].broadcast_to([P, n, E]), start=False, stop=(t == NT - 1))
            mm.then_inc(rank_psum, 1)
            for n in range(2 * NT):
                pe.wait_ge(onehot_ready, n + 1)
                nc.tensor.matmul(bank[1][:, 0:2 * NCOL], onehot[:, n % 8, :],
                                 spread[:, n, :, :].rearrange("p q s -> p (q s)"), start=(n == 0),
                                 stop=(n == 2 * NT - 1)).then_inc(onehot_used, 1)

            gu_flat = gu[:, :, :, :].rearrange("p s q n -> p (s q n)")
            dn_flat = dn[:, :, :, :].rearrange("p s q n -> p (s q n)")

            def transpose_x(s):
                pe.wait_ge(x_staged, s + 1)
                if not isinstance(s, int) or s >= 1:
                    pe.wait_ge(xT_split, s)
                for k in range(KC):
                    mm = nc.tensor.transpose(bank[7][:, k * P:(k + 1) * P], xs[:, k * P:(k + 1) * P], ident)
                mm.then_inc(xT_made, 1)

            def expand(s, par, hf, e):
                if hf == 0:
                    pe.wait_ge(xT_split, s + 1)
                    pe.wait_ge(w_split, (e + 1) * SPLITS)
                if not isinstance(s, int) or s >= 1:
                    pe.wait_ge(h_made, 2 * s + hf - 1)
                base = (e & 1) * (2 * GU)
                for k in range(KC):
                    for xp, wp in ((0, 0), (0, 1), (1, 0)):
                        for n, col in ((0, hf * HALF), (1, I + hf * HALF)):
                            mm = nc.tensor.matmul(bank[2 * hf + n][:, :], xT[:, par, xp, k, :],
                                                  gu_flat[:, bass.ds(base + (wp * GU + k * 2 * I + col), HALF)],
                                                  start=(k == 0 and xp == 0 and wp == 0), stop=(k == KC - 1 and xp == 1))
                mm.then_inc(gu_made, 1)

            def transpose_h(s, hf):
                pe.wait_ge(h_made, 2 * s + hf + 1)
                if not isinstance(s, int) or s >= 1:
                    pe.wait_ge(hT_split, 2 * s + hf - 1)
                for j in range(JH):
                    mm = nc.tensor.transpose(bank[4 + hf][:, j * P:(j + 1) * P], h[:, hf, j * P:(j + 1) * P], ident)
                mm.then_inc(hT_made, 1)

            def contract(s, hf, e):
                pe.wait_ge(hT_split, 2 * s + hf + 1)
                if hf == 0 and (not isinstance(s, int) or s >= 1):
                    pe.wait_ge(y_out, s)
                base = (e & 1) * (2 * DN)
                for j in range(JH):
                    for hp, wp in ((0, 0), (0, 1), (1, 0)):
                        mm = nc.tensor.matmul(bank[6][:, 0:D], hT[:, hf, hp, j * P:(j + 1) * P],
                                              dn_flat[:, bass.ds(base + (wp * DN + (hf * JH + j) * D), D)],
                                              start=(hf == 0 and j == 0 and hp == 0 and wp == 0),
                                              stop=(hf == 1 and j == JH - 1 and hp == 1))
                if hf == 1:
                    mm.then_inc(y_made, 1)

            def expert_of(s):
                return pe.value_load(tab[0:1, 0, bass.ds(s, 1)], min_val=0, max_val=E - 1)

            def step(s, par, first=False, ahead=1):
                e = expert_of(s)
                expand(s, par, 0, e)
                if not first:
                    e_before = expert_of(s - 1)
                    transpose_h(s - 1, 1)
                    contract(s - 1, 0, e_before)
                if ahead:
                    transpose_x(s + 1)
                expand(s, par, 1, e)
                transpose_h(s, 0)
                if not first:
                    contract(s - 1, 1, e_before)

            pe.wait_ge(tables_ready, 1)
            transpose_x(0)
            step(0, 0, first=True)
            with pe.Fori(0, (NBLK - 3) // 2) as i:
                step(i * 2 + 1, 1)
                step(i * 2 + 2, 0)
            step(NBLK - 2, 1)
            step(NBLK - 1, 0, ahead=0)
            e_last = expert_of(NBLK - 1)
            transpose_h(NBLK - 1, 1)
            contract(NBLK - 1, 0, e_last)
            contract(NBLK - 1, 1, e_last)

        @block.vector
        def _(dve):
            V = nc.vector
            n_step = [0]

            def link(ins):
                n_step[0] += 1
                ins.then_inc(dve_step, 1)
                dve.wait_ge(dve_step, n_step[0])

            def rsqrt(var, out, n):
                a, b_, y_ = nwt[:, 0, 0:n], nwt[:, 1, 0:n], nwt[:, 2, 0:n]
                link(V.tensor_scalar(a, var, EPS, None, ALU.add))
                link(V.tensor_scalar(y_.bitcast(I32), a.bitcast(I32), -0.5, MAGIC, ALU.mult, ALU.add))
                for it in range(3):
                    link(V.tensor_tensor(b_, y_, y_, ALU.mult))
                    link(V.scalar_tensor_tensor(out=b_, in0=b_, scalar=-0.5, in1=a, op0=ALU.mult, op1=ALU.mult))
                    link(V.scalar_tensor_tensor(out=(out if it == 2 else y_), in0=b_, scalar=1.5, in1=y_,
                                                op0=ALU.add, op1=ALU.mult))

            def moments(t, into):
                V.bn_stats(stats[:, t, :], x[:, t, :]).then_inc(dve_step, 1)
                n_step[0] += 1
                dve.wait_ge(dve_step, n_step[0])
                V.bn_aggr(into[:, t, :], stats[:, t, :]).then_inc(dve_step, 1)
                n_step[0] += 1

            def settle():
                dve.wait_ge(dve_step, n_step[0])

            def normalise(b):
                if b >= 2:
                    dve.wait_ge(xnT_psum, b - 1)
                for j in range(TB):
                    t = TB * b + j
                    V.tensor_scalar(xn[:, b % 2, j, :], x[:, t, :], mv[:, t, 0:1], rstd[:, t:t + 1],
                                    ALU.subtract, ALU.mult).then_inc(xn_ready, 1)

            dve.wait_ge(small_in, 16)
            raw = small[:, 0:1024].rearrange("p (c g n) -> p c g n", c=KC, g=GROUPS)
            link(V.tensor_tensor(wq[:, :, :], raw[:, :, 0, :], raw[:, :, 1, :], ALU.add))
            link(V.tensor_tensor(wq[:, :, :], wq[:, :, :], raw[:, :, 2, :], ALU.add))
            V.tensor_tensor(wq[:, :, :], wq[:, :, :], raw[:, :, 3, :], ALU.add).then_inc(wq_summed, 1)
            dve.wait_ge(x_in[0], 16)
            for t in range(TB):
                moments(t, mv)
            settle()
            rsqrt(mv[:, 0:TB, 1], rstd[:, 0:TB], TB)
            normalise(0)
            dve.wait_ge(const_in, 16)

            def rope_keys(g):
                dve.wait_ge(k_psum, g + 1)
                kr = krot[:, 4 * g:4 * g + 4, :]
                both = lambda n: c(n).rearrange("p (o a) -> p o a", o=1).broadcast_to([P, 4, A])
                V.tensor_tensor(kr, bank[2 + 2 * g][:, 0:4 * A].rearrange("p (b a) -> p b a", b=4), both("kcos"),
                                ALU.mult).then_inc(dve_step, 1)
                V.tensor_tensor(ktmp[:, :, :], bank[3 + 2 * g][:, 0:4 * A].rearrange("p (b a) -> p b a", b=4),
                                both("ksin"), ALU.mult).then_inc(dve_step, 1)
                n_step[0] += 2
                settle()
                V.tensor_tensor(kr, kr, ktmp[:, :, :], ALU.add).then_inc(krot_ready, 1)

            rope_keys(0)
            dve.wait_ge(krot_ready, 1)
            rope_keys(1)
            link(V.tensor_copy(before_bf[:, :], c("before")))
            dve.wait_ge(tanh_ready, 1)
            link(V.tensor_scalar(tg[:, 0:1], tg[:, 0:1], 1.0 / KVH, None, ALU.mult))
            for b in range(1, B):
                dve.wait_ge(x_in[b], 16)
                for j in range(TB):
                    moments(TB * b + j, mv)
            settle()
            rsqrt(mv[:, TB:NT, 1], rstd[:, TB:NT], NT - TB)

            def normalise2(b):
                if b >= 1:
                    dve.wait_ge(xn2T_psum, b)
                    dve.wait_ge(xn2_out, 16 * b)
                for j in range(TB):
                    t = TB * b + j
                    V.tensor_scalar(xn2[:, j, :], x[:, t, :], mv2[:, t, 0:1], rstd2[:, t:t + 1],
                                    ALU.subtract, ALU.mult).then_inc(xn2_ready, 1)

            for t in range(B + 2):
                if t >= 2:
                    normalise2(t - 2)
                if 1 <= t <= B:
                    b = t - 1
                    dve.wait_ge(pT_psum, 2 * b + 2)
                    if b >= 1:
                        dve.wait_ge(o_psum, b)
                    V.tensor_copy(probsT[:, 2:4, :].rearrange("a h s -> a (h s)"), bank[5][0:A, :])\
                     .then_inc(pT_dve, 1)
                if t < B:
                    dve.wait_ge(q_psum, t + 1)
                    if t >= 1:
                        dve.wait_ge(s_psum, TB * t)
                    V.tensor_tensor(qrot[:, :], bank[1][:, 0:S], c("rope"), ALU.mult).then_inc(qrot_ready, 1)
                    if t + 1 < B:
                        normalise(t + 1)
                    for j in range(TB):
                        dve.wait_ge(s_psum, TB * t + j + 1)
                        link(V.tensor_reduce(negmax[:, j, :],
                                             bank[2 + j][:, 0:KVH * A].rearrange("p (h a) -> p h a", h=KVH),
                                             AX.X, ALU.max))
                        V.tensor_scalar(negmax[:, j, :], negmax[:, j, :], -(HD ** -0.5), None,
                                        ALU.mult).then_inc(negmax_ready, 1)
                if 1 <= t <= B:
                    b = t - 1
                    dve.wait_ge(att_psum, b + 1)
                    for j in range(TB):
                        tt = TB * b + j
                        V.scalar_tensor_tensor(out=x[:, tt, :], in0=bank[7][:, j * D:(j + 1) * D], scalar=tg[:, 0:1],
                                               in1=x[:, tt, :], op0=ALU.mult, op1=ALU.add).then_inc(x2_ready, 1)
                    dve.wait_ge(x2_ready, TB * (b + 1))
                    for j in range(TB):
                        moments(TB * b + j, mv2)
                    settle()
                    rsqrt(mv2[:, TB * b:TB * b + TB, 1], rstd2[:, TB * b:TB * b + TB], TB)
                if t < B:
                    for j in range(TB):
                        dve.wait_ge(exp_done, KVH * (TB * t + j + 1))
                        link(V.reciprocal(den[:, j, :], den[:, j, :]))
                        V.tensor_tensor(probs[:, j, :, :], probs[:, j, :, :],
                                        den[:, j, :].rearrange("p (h o) -> p h o", o=1).broadcast_to([P, KVH, A]),
                                        ALU.mult).then_inc(probs_ready, 1)
                if t >= 2:
                    b = t - 2
                    dve.wait_ge(lg_psum, b + 1)
                    V.tensor_copy(logits[:, TB * b:TB * b + TB, :].rearrange("p t e -> p (t e)"),
                                  bank[6][:, S:S + TB * E]).then_inc(lg_ready, 1)

            dve.wait_ge(lg_ready, B)
            per_tile = lambda ap: ap.rearrange("p (t o) -> p t o", o=1).broadcast_to([P, NT, E])
            per_expert = lambda ap: ap.rearrange("p (o e) -> p o e", o=1).broadcast_to([P, NT, E])
            link(V.tensor_reduce(pscore[:, :], logits[:, :, :], AX.X, ALU.max))
            V.tensor_tensor(rb[:, :, :], logits[:, :, :], per_tile(pscore[:, :]), ALU.subtract).then_inc(shifted, 1)
            dve.wait_ge(rexp_ready, 1)
            for k in range(2):
                src = rexp if k == 0 else ra
                link(V.tensor_reduce(pmax[:, k, :], src[:, :, :], AX.X, ALU.max))
                link(V.tensor_tensor(rb[:, :, :], src[:, :, :], per_tile(pmax[:, k, :]), ALU.is_equal))
                link(V.tensor_tensor(rb[:, :, :], rb[:, :, :], per_expert(c("prio")), ALU.mult))
                link(V.tensor_reduce(pscore[:, :], rb[:, :, :], AX.X, ALU.max))
                link(V.tensor_tensor(pick[:, k, :, :], rb[:, :, :], per_tile(pscore[:, :]), ALU.is_equal))
                if k == 0:
                    link(V.scalar_tensor_tensor(out=ra[:, :, :], in0=pick[:, 0, :, :], scalar=-4.0,
                                                in1=rexp[:, :, :], op0=ALU.mult, op1=ALU.add))
            V.memset(chosen[:, NT:NT + 1, :], 0.0).then_inc(chosen_ready, 1)
            V.tensor_tensor(chosen[:, 0:NT, :], pick[:, 0, :, :], pick[:, 1, :, :], ALU.add).then_inc(chosen_ready, 3)
            link(V.tensor_tensor(pscore[:, :], pmax[:, 0, :], pmax[:, 1, :], ALU.add))
            link(V.reciprocal(pscore[:, :], pscore[:, :]))
            link(V.tensor_scalar(pscore[:, :], pscore[:, :], tg[:, 1:2], None, ALU.mult))
            for k in range(2):
                link(V.tensor_tensor(pmax[:, k, :], pmax[:, k, :], pscore[:, :], ALU.mult))
            dve.wait_ge(rank_psum, 1)
            link(V.tensor_copy(slotpos[:, :, :].rearrange("p t e -> p (t e)"), bank[0][:, 0:(NT + 1) * E]))
            cmp_ = rcmp[:, 0:E * 15].rearrange("p (e n) -> p e n", e=E)
            link(V.tensor_tensor(cmp_, slotpos[:, NT, :].rearrange("p (e o) -> p e o", o=1).broadcast_to([P, E, 15]),
                                 c("steps").rearrange("p (o n) -> p o n", o=1).broadcast_to([P, E, 15]), ALU.is_gt))
            link(V.tensor_reduce(nblk[:, :], cmp_, AX.X, ALU.add))
            link(V.tensor_scalar(nblk[:, :], nblk[:, :], 1.0, None, ALU.add))
            upto = c("upto").rearrange("p (e n) -> p e n", e=E)
            cum = rcmp[:, 0:E * E].rearrange("p (e n) -> p e n", e=E)
            link(V.tensor_tensor(cum, upto, nblk[:, :].rearrange("p (o e) -> p o e", o=1).broadcast_to([P, E, E]),
                                 ALU.mult))
            link(V.tensor_reduce(endblk[:, :], cum, AX.X, ALU.add))
            link(V.tensor_tensor(startslot[:, :], endblk[:, :], nblk[:, :], ALU.subtract))
            link(V.tensor_scalar(startslot[:, :], startslot[:, :], float(P), None, ALU.mult))
            link(V.tensor_tensor(ra[:, :, :], slotpos[:, 0:NT, :], per_expert(startslot[:, :]), ALU.add))
            for k in range(2):
                link(V.tensor_tensor(rb[:, :, :], pick[:, k, :, :], ra[:, :, :], ALU.mult))
                link(V.tensor_reduce(slot[:, k, :], rb[:, :, :], AX.X, ALU.add))
            link(V.tensor_copy(slot_i[:, 0, :], slot[:, :, :].rearrange("p k t -> p (k t)")))
            link(V.tensor_scalar(slot_i[:, 1, :], slot_i[:, 0, :], P - 1, None, ALU.bitwise_and))
            link(V.tensor_scalar(slot_i[:, 0, :], slot_i[:, 0, :], 7, None, ALU.arith_shift_right))
            link(V.tensor_copy(slot_f[:, :, :], slot_i[:, :, :]))
            oh = rcmp[:, :].rearrange("p (n s) -> p n s", n=2 * NT)
            link(V.tensor_tensor(oh, slot_f[:, 0, :].rearrange("p (n o) -> p n o", o=1).broadcast_to([P, 2 * NT, NCOL]),
                                 c("blocks").rearrange("p (o s) -> p o s", o=1).broadcast_to([P, 2 * NT, NCOL]),
                                 ALU.is_equal))
            for k in range(2):
                link(V.tensor_tensor(spread[:, k * NT:(k + 1) * NT, 0, :], oh[:, k * NT:(k + 1) * NT, :],
                                     c("token1").rearrange("p (t o) -> p t o", o=1).broadcast_to([P, NT, NCOL]),
                                     ALU.mult))
                link(V.tensor_tensor(spread[:, k * NT:(k + 1) * NT, 1, :], oh[:, k * NT:(k + 1) * NT, :],
                                     pmax[:, k, :].rearrange("p (t o) -> p t o", o=1).broadcast_to([P, NT, NCOL]),
                                     ALU.mult))
            for n in range(2 * NT):
                if n >= 8:
                    dve.wait_ge(onehot_used, n - 7)
                V.tensor_scalar(onehot[:, n % 8, :], c("iota"), slot_f[:, 1, n:n + 1], None,
                                ALU.is_equal).then_inc(onehot_ready, 1)
            ends = rcmp[:, 0:NCOL * E].rearrange("p (s e) -> p s e", e=E)
            link(V.tensor_tensor(ends, endblk[:, :].rearrange("p (o e) -> p o e", o=1).broadcast_to([P, NCOL, E]),
                                 c("blocks").rearrange("p (s o) -> p s o", o=1).broadcast_to([P, NCOL, E]), ALU.is_le))
            link(V.tensor_reduce(tabf[:, 0, :], ends, AX.X, ALU.add))
            link(V.tensor_scalar(tabf[:, 0, :], tabf[:, 0, :], float(E - 1), None, ALU.min))
            link(V.memset(tabf[:, 1:3, :], 0.0))
            link(V.tensor_tensor(tabf[:, 1, 1:NCOL], tabf[:, 0, 1:NCOL], tabf[:, 0, 0:NCOL - 1], ALU.is_gt))
            link(V.tensor_scalar(tabf[:, 2, :], tabf[:, 0, :], float(E - 1), None, ALU.is_lt))
            link(V.tensor_tensor(tabf[:, 1, :], tabf[:, 1, :], tabf[:, 2, :], ALU.mult))
            link(V.tensor_tensor(tabf[:, 1, :], tabf[:, 1, :], tabf[:, 0, :], ALU.mult))
            link(V.tensor_copy(tab[:, :, :], tabf[:, 0:2, :]))
            dve.wait_ge(onehot_used, 2 * NT)
            link(V.tensor_copy(idxf[:, 0, :], bank[1][:, 0:NCOL]))
            link(V.tensor_copy(wslot[:, :], bank[1][:, NCOL:2 * NCOL]))
            link(V.tensor_scalar(idxf[:, 1, :], idxf[:, 0, :], 0.0, None, ALU.is_equal))
            link(V.tensor_scalar(idxf[:, 1, :], idxf[:, 1, :], c("spare"), -1.0, ALU.mult, ALU.add))
            link(V.tensor_tensor(idxf[:, 0, :], idxf[:, 0, :], idxf[:, 1, :], ALU.add))
            V.tensor_copy(idx[:, :], idxf[:, 0, :]).then_inc(tables_ready, 1)

            def x_low(s, par):
                dve.wait_ge(xT_hi, s + 1)
                V.tensor_tensor(xT[:, par, 1, :, :].rearrange("p c t -> p (c t)"), bank[7][:, 0:D],
                                xT[:, par, 0, :, :].rearrange("p c t -> p (c t)"), ALU.subtract).then_inc(xT_split, 1)

            def product(s, hf):
                dve.wait_ge(silu_made, 2 * s + hf + 1)
                if not isinstance(s, int) or s >= 1:
                    dve.wait_ge(hT_made, 2 * s + hf - 1)
                V.tensor_tensor(h[:, hf, :], silu[:, hf, :], bank[2 * hf + 1][:, :], ALU.mult).then_inc(h_made, 1)

            def h_low(s, hf):
                dve.wait_ge(hT_hi, 2 * s + hf + 1)
                V.tensor_tensor(hT[:, hf, 1, :], bank[4 + hf][:, :], hT[:, hf, 0, :], ALU.subtract)\
                 .then_inc(hT_split, 1)

            def weigh(s):
                dve.wait_ge(y_made, s + 1)
                dve.wait_ge(y_free, s + 1)
                V.tensor_scalar(y[:, :, :].rearrange("p r d -> p (r d)")[:, bass.ds((s & (RING - 1)) * D, D)],
                                bank[6][:, 0:D], wslot[:, bass.ds(s, 1)], None, ALU.mult).then_inc(y_out, 1)

            def step(s, par, first=False, ahead=1):
                product(s, 0)
                if not first:
                    h_low(s - 1, 1)
                if ahead:
                    x_low(s + 1, 1 - par)
                product(s, 1)
                h_low(s, 0)
                if not first:
                    weigh(s - 1)

            x_low(0, 0)
            step(0, 0, first=True)
            with dve.Fori(0, (NBLK - 3) // 2) as i:
                step(i * 2 + 1, 1)
                step(i * 2 + 2, 0)
            step(NBLK - 2, 1)
            step(NBLK - 1, 0, ahead=0)
            h_low(NBLK - 1, 1)
            weigh(NBLK - 1)


def shape_constants():
    out = np.zeros((P, NCONST), np.float32)

    def put(name, value):
        a, b = CONSTS[name]
        out[:, a:b] = value

    inv = (np.float32(1.0) / np.float32(10000.0) ** (np.arange(0, HD, 2, dtype=np.float32) / np.float32(HD)))
    ang = np.arange(S, dtype=np.float32)[:, None] * inv[None, :].astype(np.float32)
    cos, sin = np.cos(ang).astype(np.float32), np.sin(ang).astype(np.float32)
    row = np.arange(P) % HR
    d = row % HD
    sign = np.where(d % 2 == 0, -1.0, 1.0).astype(np.float32)[:, None]
    put("ident", np.eye(P))
    put("rope", np.where((row < HD)[:, None], cos[:, d // 2].T, sign * sin[:, d // 2].T))
    put("kcos", cos[:A, d // 2].T)
    put("ksin", sign * sin[:A, d // 2].T)
    put("headmask", np.repeat((np.arange(P)[:, None] // HR == np.arange(KVH)[None, :]), A, axis=1))
    put("before", np.arange(P)[:, None] < np.arange(P)[None, :])
    put("iota", np.arange(P)[None, :])
    put("prio", E - np.arange(E)[None, :])
    put("steps", P * np.arange(1, 16)[None, :])
    put("upto", (np.arange(E)[None, :] <= np.arange(E)[:, None]).reshape(1, E * E))
    put("blocks", np.arange(NCOL)[None, :])
    put("token1", np.arange(NT)[None, :] * P + np.arange(P)[:, None] + 1)
    put("spare", np.arange(P)[:, None] + T + 1)
    return out


def kernel(**inputs):
    import concourse.bacc as bacc
    from concourse.bass_utils import run_bass_kernel_spmd

    x = np.ascontiguousarray(inputs["x"]).reshape(T, D)
    ctx = np.ascontiguousarray(inputs["ctx_1024"])
    Wq, Wk, Wv, Wo = (np.ascontiguousarray(inputs[f"L0_xattn_{n}"]) for n in ("Wq", "Wk", "Wv", "Wo"))
    gate = np.ascontiguousarray(inputs["L0_ffn_gate_w"])
    gup = np.ascontiguousarray(inputs["L0_ffn_gate_up_proj"])
    down = np.ascontiguousarray(inputs["L0_ffn_down_proj"])
    g2 = np.concatenate([np.ascontiguousarray(inputs["g_xattn"]), np.ascontiguousarray(inputs["g_ffn"])])

    swap = np.arange(HD) ^ 1

    def by_chunk(a):
        return a.reshape(KC, P, -1).transpose(1, 0, 2).reshape(P, -1)

    q4 = Wq.reshape(D, KVH, GROUPS, HD).transpose(0, 2, 1, 3)
    q4 = np.concatenate([q4, q4[..., swap]], axis=-1).reshape(D, -1)
    ka = np.concatenate([Wk, Wk], axis=-1).reshape(D, -1)
    kb = np.concatenate([Wk[..., swap], Wk[..., swap]], axis=-1).reshape(D, -1)
    small = np.concatenate([by_chunk(q4), by_chunk(ka), by_chunk(kb), by_chunk(Wv.reshape(D, -1)),
                            by_chunk(gate.T), np.broadcast_to(g2[None, :], (P, 2))], axis=1)
    arrays = {
        "x": x,
        "ctxT": ctx.reshape(B * A, KC, P).transpose(2, 1, 0),
        "small": small,
        "wo": Wo,
        "gu": gup.transpose(0, 2, 1).reshape(E, KC, P, 2 * I).transpose(0, 2, 1, 3).reshape(E, P, GU),
        "dn": down.transpose(0, 2, 1).reshape(E, I // P, P, D).transpose(0, 2, 1, 3).reshape(E, P, DN),
        "consts": shape_constants(),
    }
    arrays = {k: np.ascontiguousarray(a) for k, a in arrays.items()}
    nc = bacc.Bacc("TRN2", target_bir_lowering=False, num_devices=1)
    aps = [nc.dram_tensor(f"in_{k}", a.shape, mybir.dt.from_np(a.dtype), kind="ExternalInput").ap() for k, a in arrays.items()]
    out = nc.dram_tensor("out", (T + P, D), F32, kind="ExternalOutput").ap()
    build_program(nc, *aps, out)
    r = run_bass_kernel_spmd(nc, [{f"in_{k}": a for k, a in arrays.items()}], core_ids=[0])
    return r.results[0]["out"][:T].reshape(B, S, D)
```

```python
from contextlib import ExitStack

import numpy as np
import concourse.bass as bass
from concourse import mybir

F32 = mybir.dt.float32
F32R = mybir.dt.float32r
BF16 = mybir.dt.bfloat16
I32 = mybir.dt.int32
ALU = mybir.AluOpType
ACT = mybir.ActivationFunctionType
AX = mybir.AxisListType

P = 128
B, S, D = 8, 256, 256
A = 120
KVH, GROUPS, HD = 4, 4, 16
E, I = 8, 1024
T = B * S
NT = T // P
TB = S // P
KC = D // P
HR = 2 * HD
EPS = 1e-5
NBLK = (2 * T + E * (P - 1)) // P
NCOL = NBLK + 1
HALF = I // 2
JH = HALF // P
GU = KC * 2 * I
DN = (I // P) * D
RING = 4
PIECE = GU // 2
assert DN == PIECE

CONSTS = {}


def _const_columns():
    at = 0
    for name, n in (("ident", P), ("rope", S), ("kcos", A), ("ksin", A), ("headmask", KVH * A),
                    ("before", P), ("iota", P), ("prio", E), ("steps", 15), ("upto", E * E),
                    ("blocks", NCOL), ("token1", NT), ("spare", 1), ("follow", E)):
        CONSTS[name] = (at, at + n)
        at += n
    return at


NCONST = _const_columns()
WSMALL = {"wq": (0, 1024), "wka": (1024, 1280), "wkb": (1280, 1536), "wv": (1536, 1664),
          "gate": (1664, 1680), "tanh_in": (1680, 1682)}
NSMALL = 1682


def build_program(nc, x_d, ctx_d, small_d, wo_d, gu_d, dn_d, const_d, out_d):
    xn2_d = nc.dram_tensor("xn2_scratch", (T + P, D), F32, kind="Internal").ap()
    ctx = ExitStack()
    with ctx:
        def sb(name, shape, dt=F32):
            return ctx.enter_context(nc.sbuf_tensor(name, shape, dt))

        def sem(name):
            return ctx.enter_context(nc.semaphore(name))

        x = sb("x", [P, NT, D])
        const = sb("const", [P, NCONST])
        small = sb("small", [P, NSMALL])
        raw_wq = small[:, 0:1024].rearrange("p (c g n) -> p c g n", c=KC, g=GROUPS)
        wq = raw_wq[:, :, 0, :]
        wo = sb("wo", [HD, D])
        area = sb("area", [P, 3840 + KVH * S])
        ctxT = area[:, 0:KC * B * A].rearrange("p (k n) -> p k n", k=KC)
        krot = area[:, 1920:1920 + B * A].rearrange("p (b a) -> p b a", b=B)
        kbd = area[:, 2880:2880 + 2 * KVH * A].rearrange("p (q h a) -> p q h a", q=2, h=KVH)
        rcmp = area[:, 0:2 * NT * NCOL]
        v = sb("v", [A, B * KVH * HD])
        stats = sb("stats", [P, NT, 6])
        mv = sb("mv", [P, NT, 2])
        mv2 = sb("mv2", [P, NT, 2])
        rstd = sb("rstd", [P, NT])
        rstd2 = sb("rstd2", [P, NT])
        vareps = sb("vareps", [P, 2, TB])
        expo = sb("expo", [P, 1])
        xn = sb("xn", [P, 2, TB, D])
        xnT = sb("xnT", [P, KC, S])
        qrot = sb("qrot", [P, S])
        probs = sb("probs", [P, TB, KVH, A])
        ktmp = probs[:, 0, :, :]
        negmax = sb("negmax", [P, TB, KVH])
        den = sb("den", [P, TB, KVH])
        probsT = area[0:A, 3840:3840 + KVH * S].rearrange("a (h s) -> a h s", h=KVH)
        oT = sb("oT", [HD, S])
        xn2 = sb("xn2", [P, TB, D])
        xn2T = sb("xn2T", [P, KC, S])
        tg = sb("tg", [P, 2])
        zrow = xn2T[:, 0, :]
        logits = sb("logits", [P, NT, E])
        ra, rb, rexp = (small[:, n * NT * E:(n + 1) * NT * E].rearrange("p (t e) -> p t e", e=E) for n in range(3))
        pick = small[:, 3 * NT * E:5 * NT * E].rearrange("p (k t e) -> p k t e", k=2, e=E)
        pmax = sb("pmax", [P, 2, NT])
        pscore = sb("pscore", [P, NT])
        chosen = sb("chosen", [P, NT + 1, E], BF16)
        before_bf = sb("before_bf", [P, P], BF16)
        ones_bf = sb("ones_bf", [P, P], BF16)
        slotpos = sb("slotpos", [P, NT + 1, E])
        nblk = sb("nblk", [P, E])
        endblk = sb("endblk", [P, E])
        rank = sb("rank", [P, 2 * NT])
        rank_i = sb("rank_i", [P, 2, 2 * NT], I32)
        slot_f = sb("slot_f", [P, 2, 2 * NT])
        wslot = sb("wslot", [P, NCOL])
        table_area = area[:, 2 * NT * NCOL:3 * NT * NCOL]
        idxf = table_area[:, NCOL * E:NCOL * (E + 2)].rearrange("p (n s) -> p n s", n=2)
        idx = sb("idx", [P, NCOL], I32)
        wparts = sb("wparts", [P, 2, 2 * NT])
        startblk = sb("startblk", [P, E])
        tabf = table_area[:, NCOL * (E + 2):NCOL * (E + 6)].rearrange("p (n s) -> p n s", n=4)
        tab = sb("tab", [P, 4, NCOL], I32)
        idx_g = sb("idx_g", [P, 1], I32)
        idx_s = sb("idx_s", [P, 1], I32)
        wraw = sb("wraw", [P, GU + DN])
        gu = sb("gu", [P, 2, 2, GU], F32R)
        dn = sb("dn", [P, 2, 2, DN], F32R)
        late = x[:, :, :].rearrange("p t d -> p (t d)")
        xg = late[:, 0:RING * D].rearrange("p (r d) -> p r d", r=RING)
        y = late[:, RING * D:2 * RING * D].rearrange("p (r d) -> p r d", r=RING)
        silu = late[:, 2 * RING * D:2 * RING * D + I].rearrange("p (q n) -> p q n", q=2)
        h = late[:, 2 * RING * D + I:2 * RING * D + 2 * I].rearrange("p (q n) -> p q n", q=2)
        xs = xn[:, 0, 0, :]
        xT = sb("xT", [P, 2, 2, KC, P], F32R)
        hT = sb("hT", [P, 2, 2, JH * P], F32R)
        n_oh = 2 * NT - 8
        oh_hT = hT[:, :, :, :].rearrange("p a b (n q) -> p (a b n) q", q=P)
        oh_xT = xT[:, :, :, :, :].rearrange("p a b c q -> p (a b c) q")
        oh_more = sb("oh_more", [P, 8, P], F32R)
        onehot = [oh_hT[:, n, :] for n in range(16)] + [oh_more[:, n, :] for n in range(8)] + \
                 [oh_xT[:, n, :] for n in range(8)]
        spread = dn[:, 1, :, :].rearrange("p q n -> p (q n)")[:, 0:2 * NT * 3 * NCOL]\
            .rearrange("p (n q s) -> p n q s", n=2 * NT, q=3)
        bank = [ctx.enter_context(nc.psum_tensor(f"bank{i}", [P, 512], F32)) for i in range(8)]

        def c(name, n=P):
            a, b = CONSTS[name]
            return const[0:n, a:b]

        ident = c("ident")

        const_in, small_in, wo_in, ctx_in = (sem(n) for n in ("const_in", "small_in", "wo_in", "ctx_in"))
        x_in = [sem(f"x_in{b}") for b in range(B)]
        dve_step, act_step, pool_step = sem("dve_step"), sem("act_step"), sem("pool_step")
        wq_summed, k_psum, krot_ready, kbd_ready, v_psum, v_ready, tanh_ready = (
            sem(n) for n in ("wq_summed", "k_psum", "krot_ready", "kbd_ready", "v_psum", "v_ready", "tanh_ready"))
        xn_ready, xnT_psum, xnT_ready, q_psum, qrot_ready, s_psum, negmax_ready, exp_done, probs_ready = (
            sem(n) for n in ("xn_ready", "xnT_psum", "xnT_ready", "q_psum", "qrot_ready", "s_psum",
                             "negmax_ready", "exp_done", "probs_ready"))
        pT_psum, pT_act, pT_dve, o_psum, oT_ready, att_psum, x2_ready = (
            sem(n) for n in ("pT_psum", "pT_act", "pT_dve", "o_psum", "oT_ready", "att_psum", "x2_ready"))
        xn2_ready, xn2T_psum, xn2T_ready, lg_psum, lg_ready = (
            sem(n) for n in ("xn2_ready", "xn2T_psum", "xn2T_ready", "lg_psum", "lg_ready"))
        out_init, xn2_out, zrow_ready, zero_xn2, zero_out = (
            sem(n) for n in ("out_init", "xn2_out", "zrow_ready", "zero_xn2", "zero_out"))
        shifted, rexp_ready, chosen_ready, rank_psum, onehot_ready, onehot_used, slots_psum, tables_ready = (
            sem(n) for n in ("shifted", "rexp_ready", "chosen_ready", "rank_psum", "onehot_ready", "onehot_used",
                             "slots_psum", "tables_ready"))
        w_in = [sem(f"w_in{p}") for p in range(3)]
        w_hi, w_lo = sem("w_hi"), sem("w_lo")
        moments1, moments2, rstd_ready, rstd2_ready, oh_block, idx_ready = (
            sem(n) for n in ("moments1", "moments2", "rstd_ready", "rstd2_ready", "oh_block", "idx_ready"))
        row_ready, spread_tok = sem("row_ready"), sem("spread_tok")
        index_settled = sem("index_settled")
        idx_g_ready, idx_s_ready, x_gathered, y_added, y_free = (
            sem(n) for n in ("idx_g_ready", "idx_s_ready", "x_gathered", "y_added", "y_free"))
        x_staged, xT_made, xT_hi, xT_split = (sem(n) for n in ("x_staged", "xT_made", "xT_hi", "xT_split"))
        gu_made, silu_made, h_made, hT_made, hT_hi, hT_split, y_made, y_out = (
            sem(n) for n in ("gu_made", "silu_made", "h_made", "hT_made", "hT_hi", "hT_split", "y_made", "y_out"))

        block = ctx.enter_context(nc.Block())

        def gu_part(where, part, col, n):
            flat = gu[:, :, :, :].rearrange("p s q n -> p (s q n)")
            return flat[:, bass.ds(where * (2 * GU) + (part * GU + col), n)]

        def dn_part(where, part, col, n):
            flat = dn[:, :, :, :].rearrange("p s q n -> p (s q n)")
            return flat[:, bass.ds(where * (2 * DN) + (part * DN + col), n)]

        def piece_of(where, part, p):
            return gu_part(where, part, p * PIECE, PIECE) if p < 2 else dn_part(where, part, 0, DN)

        @block.sync
        def _(sp):
            sp.dma_start(small[:, :], small_d).then_inc(small_in, 16)
            sp.dma_start(ctxT[:, :, :], ctx_d).then_inc(ctx_in, 16)
            sp.dma_start(const[:, :], const_d).then_inc(const_in, 16)
            x_v = x_d.rearrange("(t p) d -> p t d", p=P)
            for b in range(B):
                sp.dma_start(x[:, TB * b:TB * b + TB, :], x_v[:, TB * b:TB * b + TB, :]).then_inc(x_in[b], 16)
            sp.dma_start(wo[:, :], wo_d).then_inc(wo_in, 16)

            def load_piece(q):
                e, p = divmod(q, 3)
                if e >= 1:
                    sp.wait_ge(w_lo, q - 2)
                src = gu_d[e][:, p * PIECE:(p + 1) * PIECE] if p < 2 else dn_d[e]
                sp.dma_start(wraw[:, p * PIECE:(p + 1) * PIECE], src).then_inc(w_in[p], 16)

            for q in range(3):
                load_piece(q)
            sp.wait_ge(zrow_ready, 1)
            sp.dma_start(out_d[T:T + P, :], zrow).then_inc(zero_out, 16)
            sp.dma_start(xn2_d[T:T + P, :], zrow).then_inc(zero_xn2, 16)
            out_v = out_d[0:T, :].rearrange("(t p) d -> p t d", p=P)
            xn2_v = xn2_d[0:T, :].rearrange("(t p) d -> p t d", p=P)
            for b in range(B):
                sp.wait_ge(x2_ready, TB * (b + 1))
                sp.dma_start(out_v[:, TB * b:TB * b + TB, :], x[:, TB * b:TB * b + TB, :]).then_inc(out_init, 16)
                sp.wait_ge(xn2_ready, TB * (b + 1))
                sp.dma_start(xn2_v[:, TB * b:TB * b + TB, :], xn2[:, :, :]).then_inc(xn2_out, 16)
                if 2 <= b <= 4:
                    load_piece(b + 1)
            for q in range(6, 3 * E):
                load_piece(q)
            sp.wait_ge(out_init, 16 * B)
            sp.wait_ge(zero_out, 16)
            sp.wait_ge(y_added, 16 * NBLK)

        @block.gpsimd
        def _(pool):
            nc.gpsimd.memset(zrow, 0.0).then_inc(zrow_ready, 1)
            nc.gpsimd.memset(ones_bf[:, :], 1.0).then_inc(pool_step, 1)
            nc.gpsimd.memset(expo[:, :], -0.5).then_inc(zrow_ready, 1)
            pool.sem_inc(y_free, RING)

            def split_low(e, p):
                pool.wait_ge(w_hi, 3 * e + (p + 1))
                where = e & 1
                nc.gpsimd.tensor_tensor(piece_of(where, 1, p), wraw[:, p * PIECE:(p + 1) * PIECE],
                                        piece_of(where, 0, p), ALU.subtract).then_inc(w_lo, 1)

            n_step = [1]

            def rsqrt(done, b, var, out, sig):
                pool.wait_ge(done, TB * (b + 1))
                n_step[0] += 1
                tmp = vareps[:, n_step[0] % 2, :]
                nc.gpsimd.tensor_scalar(tmp, var[:, TB * b:TB * b + TB, 1], EPS, None, ALU.add).then_inc(pool_step, 1)
                pool.wait_ge(pool_step, n_step[0])
                nc.gpsimd.tensor_tensor(out[:, TB * b:TB * b + TB], tmp, expo[:, 0:1].broadcast_to([P, TB]),
                                        ALU.pow).then_inc(sig, 1)
                pool.wait_ge(sig, b + 1)

            def spread_keys(b):
                pool.wait_ge(krot_ready, 2)
                if b >= 2:
                    pool.wait_ge(s_psum, TB * (b - 1))
                mask = c("headmask").rearrange("p (h a) -> p h a", h=KVH)
                nc.gpsimd.tensor_tensor(kbd[:, b % 2, :, :],
                                        krot[:, b, :].rearrange("p (o a) -> p o a", o=1).broadcast_to([P, KVH, A]),
                                        mask, ALU.mult).then_inc(kbd_ready, 1)

            pool.wait_ge(zrow_ready, 2)
            rsqrt(moments1, 0, mv, rstd, rstd_ready)
            pool.wait_ge(const_in, 16)
            spread_keys(0)
            rsqrt(moments1, 1, mv, rstd, rstd_ready)
            spread_keys(1)
            rsqrt(moments1, 2, mv, rstd, rstd_ready)
            for t in range(B + 1):
                if t + 3 < B:
                    rsqrt(moments1, t + 3, mv, rstd, rstd_ready)
                if t + 2 < B:
                    spread_keys(t + 2)
                if t >= 1:
                    rsqrt(moments2, t - 1, mv2, rstd2, rstd2_ready)
                if 1 <= t <= 5:
                    split_low(*divmod(t - 1, 3))
            pool.wait_ge(row_ready, 1)
            for n in range(8):
                nc.gpsimd.tensor_scalar(oh_xT[:, n, :], c("iota"), slot_f[:, 1, n_oh + n:n_oh + n + 1], None,
                                        ALU.is_equal).then_inc(pool_step, 1)
            pool.wait_ge(oh_block, 1)
            oh = rcmp.rearrange("p (n s) -> p n s", n=2 * NT)
            for k in range(2):
                nc.gpsimd.tensor_tensor(spread[:, k * NT:(k + 1) * NT, 0, :], oh[:, k * NT:(k + 1) * NT, :],
                                        c("token1").rearrange("p (t o) -> p t o", o=1).broadcast_to([P, NT, NCOL]),
                                        ALU.mult).then_inc(spread_tok, 1)

            def gather(g, r):
                nc.gpsimd.tensor_copy(idx_g[:, :], idx[:, bass.ds(g, 1)]).then_inc(idx_g_ready, 1)
                pool.wait_ge(idx_g_ready, g + 1)
                pool.sem_inc(index_settled, 1)
                nc.gpsimd.indirect_dma_start(
                    out=xg[:, r, :], out_offset=None, in_=xn2_d,
                    in_offset=bass.IndirectOffsetOnAxis(ap=idx_g[:, :], axis=0)).then_inc(x_gathered, 16)

            def scatter(n, r):
                pool.wait_ge(y_out, n + 1)
                nc.gpsimd.tensor_copy(idx_s[:, :], idx[:, bass.ds(n, 1)]).then_inc(idx_s_ready, 1)
                pool.wait_ge(idx_s_ready, n + 1)
                pool.sem_inc(index_settled, 1)
                nc.gpsimd.indirect_dma_start(
                    out=out_d, out_offset=bass.IndirectOffsetOnAxis(ap=idx_s[:, :], axis=0),
                    in_=y[:, r, :], in_offset=None, compute_op=ALU.add).then_inc(y_added, 16)

            def next_pieces(s):
                for p in range(3):
                    e = pool.value_load(tab[0:1, p + 1, bass.ds(s, 1)], min_val=0, max_val=E - 2)
                    with pool.If(e > 0):
                        split_low(e + 1, p)

            def step(s, r, ahead=True):
                scatter(s - 1, r)
                if ahead:
                    pool.wait_ge(x_gathered, 16 * (s + 3))
                    pool.wait_ge(x_staged, s)
                    gather(s + 3, r)
                next_pieces(s)
                pool.wait_ge(y_added, 16 * s)
                pool.sem_inc(y_free, 1)

            pool.wait_ge(idx_ready, 1)
            pool.wait_ge(xn2_out, 16 * B)
            pool.wait_ge(zero_xn2, 16)
            pool.wait_ge(zero_out, 16)
            pool.wait_ge(out_init, 16 * B)
            for g in range(RING):
                if g >= 1:
                    pool.wait_ge(x_gathered, 16 * g)
                gather(g, g)
            split_low(1, 2)
            pool.wait_ge(tables_ready, 1)
            LOOPED = (NBLK - 1 - 2) // RING
            with pool.Fori(0, LOOPED) as i:
                for u in range(RING):
                    step(i * RING + (u + 1), u)
            for s in range(LOOPED * RING + 1, NBLK):
                step(s, (s - 1) % RING, ahead=False)
            scatter(NBLK - 1, (NBLK - 1) % RING)

        @block.scalar
        def _(act):
            act.wait_ge(small_in, 16)
            a0, a1 = WSMALL["tanh_in"]
            nc.scalar.activation(tg[:, :], small[:, a0:a1], ACT.Tanh).then_inc(tanh_ready, 1)

            def split_high(e, p):
                act.wait_ge(w_in[p], (e + 1) * 16)
                where = e & 1
                nc.scalar.activation(piece_of(where, 0, p), wraw[:, p * PIECE:(p + 1) * PIECE],
                                     ACT.Copy).then_inc(w_hi, 1)

            act.wait_ge(v_psum, 1)
            nc.scalar.activation(v[:, :], bank[7][0:A, :], ACT.Copy).then_inc(v_ready, 1)

            def copy_xnT(b):
                act.wait_ge(xnT_psum, b + 1)
                if b >= 1:
                    act.wait_ge(q_psum, b)
                nc.scalar.activation(xnT[:, :, :].rearrange("p c s -> p (c s)"), bank[0][:, :],
                                     ACT.Copy).then_inc(xnT_ready, 1)

            def exponentials(b, j):
                act.wait_ge(negmax_ready, TB * b + j + 1)
                if b >= 1:
                    act.wait_ge(pT_psum, 2 * b)
                for hh in range(KVH):
                    nc.scalar.activation(probs[:, j, hh, :], bank[2 + j][:, hh * A:(hh + 1) * A], ACT.Exp,
                                         bias=negmax[:, j, hh:hh + 1], scale=HD ** -0.5,
                                         accum_out=den[:, j, hh:hh + 1]).then_inc(exp_done, 1)

            copy_xnT(0)
            for t in range(B + 2):
                if t + 1 < B:
                    copy_xnT(t + 1)
                if t < B:
                    exponentials(t, 0)
                if 1 <= t <= B:
                    b = t - 1
                    act.wait_ge(o_psum, b + 1)
                    if b >= 1:
                        act.wait_ge(att_psum, b)
                    nc.scalar.activation(oT[:, :], bank[6][0:HD, 0:S], ACT.Copy).then_inc(oT_ready, 1)
                if t < B:
                    exponentials(t, 1)
                if t >= 2:
                    b = t - 2
                    act.wait_ge(xn2T_psum, b + 1)
                    if b >= 1:
                        act.wait_ge(lg_psum, b)
                    else:
                        act.wait_ge(zero_out, 16)
                        act.wait_ge(zero_xn2, 16)
                    nc.scalar.activation(xn2T[:, :, :].rearrange("p c s -> p (c s)"), bank[0][:, :],
                                         ACT.Copy).then_inc(xn2T_ready, 1)
                if t < B:
                    act.wait_ge(pT_psum, 2 * t + 1)
                    if t >= 1:
                        act.wait_ge(o_psum, t)
                    nc.scalar.activation(probsT[:, 0:2, :].rearrange("a h s -> a (h s)"), bank[4][0:A, :],
                                         ACT.Copy).then_inc(pT_act, 1)
                if 1 <= t <= 5:
                    split_high(*divmod(t - 1, 3))
            act.wait_ge(shifted, 1)
            nc.scalar.activation(rexp[:, :, :], rb[:, :, :], ACT.Exp).then_inc(rexp_ready, 1)

            def stage(s):
                act.wait_ge(x_gathered, 16 * (s + 1))
                nc.scalar.activation(xs[:, :], xg[:, :, :].rearrange("p r d -> p (r d)")[:, bass.ds((s & (RING - 1)) * D, D)],
                                     ACT.Copy).then_inc(x_staged, 1)

            def x_high(s, par):
                act.wait_ge(xT_made, s + 1)
                nc.scalar.activation(xT[:, par, 0, :, :].rearrange("p c t -> p (c t)"), bank[7][:, 0:D],
                                     ACT.Copy).then_inc(xT_hi, 1)

            def gate(s, hf):
                act.wait_ge(gu_made, 2 * s + hf + 1)
                if not isinstance(s, int) or s >= 1:
                    act.wait_ge(h_made, 2 * s + hf - 1)
                nc.scalar.activation(silu[:, hf, :], bank[2 * hf][:, :], ACT.Silu).then_inc(silu_made, 1)

            def h_high(s, hf):
                act.wait_ge(hT_made, 2 * s + hf + 1)
                nc.scalar.activation(hT[:, hf, 0, :], bank[4 + hf][:, :], ACT.Copy).then_inc(hT_hi, 1)

            def next_pieces(s):
                for p in range(3):
                    e = act.value_load(tab[0:1, p + 1, bass.ds(s, 1)], min_val=0, max_val=E - 2)
                    with act.If(e > 0):
                        act.wait_ge(y_made, s)
                        split_high(e + 1, p)

            def step(s, par, first=False, ahead=2):
                gate(s, 0)
                if not first:
                    h_high(s - 1, 1)
                if ahead >= 1:
                    x_high(s + 1, 1 - par)
                if ahead >= 2:
                    stage(s + 2)
                gate(s, 1)
                h_high(s, 0)
                if not first:
                    next_pieces(s)

            stage(0)
            x_high(0, 0)
            stage(1)
            act.wait_ge(tables_ready, 1)
            split_high(1, 2)
            step(0, 0, first=True)
            with act.Fori(0, (NBLK - 3) // 2) as i:
                step(i * 2 + 1, 1)
                step(i * 2 + 2, 0)
            step(NBLK - 2, 1, ahead=1)
            step(NBLK - 1, 0, ahead=0)
            h_high(NBLK - 1, 1)

        @block.tensor
        def _(pe):
            wka = small[:, 1024:1280].rearrange("p (c n) -> p c n", c=KC)
            wkb = small[:, 1280:1536].rearrange("p (c n) -> p c n", c=KC)
            wv = small[:, 1536:1664].rearrange("p (c n) -> p c n", c=KC)
            gw = small[:, 1664:1680].rearrange("p (c n) -> p c n", c=KC)
            pe.wait_ge(small_in, 16)
            pe.wait_ge(ctx_in, 16)
            for g in range(2):
                for n, w in enumerate((wka, wkb)):
                    for k in range(KC):
                        mm = nc.tensor.matmul(bank[2 + 2 * g + n][:, 0:4 * A], w[:, k, :],
                                              ctxT[:, k, 4 * A * g:4 * A * (g + 1)], start=(k == 0), stop=(k == KC - 1))
                mm.then_inc(k_psum, 1)
            for b in range(B):
                for k in range(KC):
                    mm = nc.tensor.matmul(bank[7][0:A, b * 64:(b + 1) * 64], ctxT[:, k, b * A:(b + 1) * A],
                                          wv[:, k, :], start=(k == 0), stop=(k == KC - 1))
            mm.then_inc(v_psum, 1)
            pe.wait_ge(const_in, 16)
            pe.wait_ge(wq_summed, 1)

            def transpose_xn(b):
                pe.wait_ge(xn_ready, TB * (b + 1))
                if b >= 4:
                    pe.wait_ge(xn2T_ready, b - 3)
                for j in range(TB):
                    for k in range(KC):
                        mm = nc.tensor.transpose(bank[0][:, k * S + j * P:k * S + (j + 1) * P],
                                                 xn[:, b % 2, j, k * P:(k + 1) * P], ident)
                mm.then_inc(xnT_psum, 1)

            def project_q(b):
                pe.wait_ge(xnT_ready, b + 1)
                if b >= 1:
                    pe.wait_ge(qrot_ready, b)
                for k in range(KC):
                    mm = nc.tensor.matmul(bank[1][:, 0:S], raw_wq[:, k, 0, :], xnT[:, k, :],
                                          start=(k == 0), stop=(k == KC - 1))
                mm.then_inc(q_psum, 1)

            transpose_xn(0)
            project_q(0)
            for t in range(B + 3):
                if t < B:
                    pe.wait_ge(qrot_ready, t + 1)
                    pe.wait_ge(kbd_ready, t + 1)
                    if t >= 1:
                        pe.wait_ge(exp_done, TB * KVH * t)
                    for j in range(TB):
                        nc.tensor.matmul(bank[2 + j][:, 0:KVH * A], qrot[:, j * P:(j + 1) * P],
                                         kbd[:, t % 2, :, :].rearrange("p h a -> p (h a)"),
                                         start=True, stop=True).then_inc(s_psum, 1)
                if t + 1 < B:
                    transpose_xn(t + 1)
                if 1 <= t <= B:
                    b = t - 1
                    pe.wait_ge(pT_act, b + 1)
                    pe.wait_ge(pT_dve, b + 1)
                    pe.wait_ge(v_ready, 1)
                    if b >= 3:
                        pe.wait_ge(lg_ready, b - 2)
                    for hh in range(KVH):
                        mm = nc.tensor.matmul(bank[6][0:HD, 0:S], v[:, b * 64 + hh * HD:b * 64 + (hh + 1) * HD],
                                              probsT[:, hh, :], start=(hh == 0), stop=(hh == KVH - 1))
                    mm.then_inc(o_psum, 1)
                if t + 1 < B:
                    project_q(t + 1)
                if 1 <= t <= B:
                    b = t - 1
                    pe.wait_ge(oT_ready, b + 1)
                    if b == 0:
                        pe.wait_ge(wo_in, 16)
                    else:
                        pe.wait_ge(x2_ready, TB * b)
                    for j in range(TB):
                        mm = nc.tensor.matmul(bank[7][:, j * D:(j + 1) * D], oT[:, j * P:(j + 1) * P], wo[:, :],
                                              start=True, stop=True)
                    mm.then_inc(att_psum, 1)
                if t >= 3:
                    b = t - 3
                    pe.wait_ge(xn2T_ready, b + 1)
                    if b >= 1:
                        pe.wait_ge(lg_ready, b)
                    for j in range(TB):
                        for k in range(KC):
                            mm = nc.tensor.matmul(bank[6][:, S + j * E:S + (j + 1) * E],
                                                  xn2T[:, k, j * P:(j + 1) * P], gw[:, k, :],
                                                  start=(k == 0), stop=(k == KC - 1))
                    mm.then_inc(lg_psum, 1)
                if 2 <= t < B + 2:
                    b = t - 2
                    pe.wait_ge(xn2_ready, TB * (b + 1))
                    if b >= 1:
                        pe.wait_ge(xn2T_ready, b)
                    for j in range(TB):
                        for k in range(KC):
                            mm = nc.tensor.transpose(bank[0][:, k * S + j * P:k * S + (j + 1) * P],
                                                     xn2[:, j, k * P:(k + 1) * P], ident)
                    mm.then_inc(xn2T_psum, 1)
                if t < B:
                    pe.wait_ge(probs_ready, TB * (t + 1))
                    if t == 0:
                        pe.wait_ge(krot_ready, 2)
                    else:
                        pe.wait_ge(pT_act, t)
                        pe.wait_ge(pT_dve, t)
                    for g in range(2):
                        for hh in range(2):
                            for j in range(TB):
                                mm = nc.tensor.transpose(bank[4 + g][0:A, hh * S + j * P:hh * S + (j + 1) * P],
                                                         probs[:, j, 2 * g + hh, :], ident)
                        mm.then_inc(pT_psum, 1)

            ONEHOT0 = 1 + 2 * B
            pe.wait_ge(chosen_ready, 4)
            pe.wait_ge(pool_step, 1)
            flat = chosen[:, :, :].rearrange("p t e -> p (t e)")
            nc.tensor.matmul(bank[0][:, 0:(NT + 1) * E], before_bf[:, :], flat, start=True, stop=False)
            for t in range(NT):
                n = NT - t
                mm = nc.tensor.matmul(bank[0][:, (t + 1) * E:(NT + 1) * E], ones_bf[:, :],
                                      chosen[:, t:t + 1, :].broadcast_to([P, n, E]), start=False, stop=(t == NT - 1))
            mm.then_inc(rank_psum, 1)
            for n in range(2 * NT):
                if n < n_oh:
                    pe.wait_ge(onehot_ready, n // 8 + 1)
                else:
                    pe.wait_ge(pool_step, ONEHOT0 + n - n_oh + 1)
                if n == 0:
                    pe.wait_ge(spread_tok, 4)
                nc.tensor.matmul(bank[1][:, 0:3 * NCOL], onehot[n],
                                 spread[:, n, :, :].rearrange("p q s -> p (q s)"), start=(n == 0),
                                 stop=(n == 2 * NT - 1)).then_inc(onehot_used, 1)

            def transpose_x(s):
                pe.wait_ge(x_staged, s + 1)
                if not isinstance(s, int) or s >= 1:
                    pe.wait_ge(xT_split, s)
                for k in range(KC):
                    mm = nc.tensor.transpose(bank[7][:, k * P:(k + 1) * P], xs[:, k * P:(k + 1) * P], ident)
                mm.then_inc(xT_made, 1)

            def expand(s, par, hf, e):
                if hf == 0:
                    pe.wait_ge(xT_split, s + 1)
                    pe.wait_ge(w_lo, (e + 1) * 3)
                if not isinstance(s, int) or s >= 1:
                    pe.wait_ge(h_made, 2 * s + hf - 1)
                where = e & 1
                for k in range(KC):
                    for xp, wp in ((0, 0), (0, 1), (1, 0)):
                        for n, col in ((0, hf * HALF), (1, I + hf * HALF)):
                            mm = nc.tensor.matmul(bank[2 * hf + n][:, :], xT[:, par, xp, k, :],
                                                  gu_part(where, wp, k * 2 * I + col, HALF),
                                                  start=(k == 0 and xp == 0 and wp == 0), stop=(k == KC - 1 and xp == 1))
                mm.then_inc(gu_made, 1)

            def transpose_h(s, hf):
                pe.wait_ge(h_made, 2 * s + hf + 1)
                if not isinstance(s, int) or s >= 1:
                    pe.wait_ge(hT_split, 2 * s + hf - 1)
                for j in range(JH):
                    mm = nc.tensor.transpose(bank[4 + hf][:, j * P:(j + 1) * P], h[:, hf, j * P:(j + 1) * P], ident)
                mm.then_inc(hT_made, 1)

            def contract(s, hf, e):
                pe.wait_ge(hT_split, 2 * s + hf + 1)
                if hf == 0 and (not isinstance(s, int) or s >= 1):
                    pe.wait_ge(y_out, s)
                where = e & 1
                for j in range(JH):
                    for hp, wp in ((0, 0), (0, 1), (1, 0)):
                        mm = nc.tensor.matmul(bank[6][:, 0:D], hT[:, hf, hp, j * P:(j + 1) * P],
                                              dn_part(where, wp, (hf * JH + j) * D, D),
                                              start=(hf == 0 and j == 0 and hp == 0 and wp == 0),
                                              stop=(hf == 1 and j == JH - 1 and hp == 1))
                if hf == 1:
                    mm.then_inc(y_made, 1)

            def expert_of(s):
                return pe.value_load(tab[0:1, 0, bass.ds(s, 1)], min_val=0, max_val=E - 1)

            def step(s, par, first=False, ahead=1):
                e = expert_of(s)
                expand(s, par, 0, e)
                if not first:
                    e_before = expert_of(s - 1)
                    transpose_h(s - 1, 1)
                    contract(s - 1, 0, e_before)
                if ahead:
                    transpose_x(s + 1)
                expand(s, par, 1, e)
                transpose_h(s, 0)
                if not first:
                    contract(s - 1, 1, e_before)

            pe.wait_ge(idx_ready, 1)
            transpose_x(0)
            step(0, 0, first=True)
            with pe.Fori(0, (NBLK - 3) // 2) as i:
                step(i * 2 + 1, 1)
                step(i * 2 + 2, 0)
            step(NBLK - 2, 1)
            step(NBLK - 1, 0, ahead=0)
            e_last = expert_of(NBLK - 1)
            transpose_h(NBLK - 1, 1)
            contract(NBLK - 1, 0, e_last)
            contract(NBLK - 1, 1, e_last)

        @block.vector
        def _(dve):
            V = nc.vector
            n_step = [0]

            def link(ins):
                n_step[0] += 1
                ins.then_inc(dve_step, 1)
                dve.wait_ge(dve_step, n_step[0])

            def moments(b, into, sig):
                for t in range(TB * b, TB * b + TB):
                    V.bn_stats(stats[:, t, :], x[:, t, :]).then_inc(dve_step, 1)
                    n_step[0] += 1
                for t in range(TB * b, TB * b + TB):
                    dve.wait_ge(dve_step, n_step[0] - TB + 1 + t - TB * b)
                    V.bn_aggr(into[:, t, :], stats[:, t, :]).then_inc(sig, 1)

            def settle():
                dve.wait_ge(dve_step, n_step[0])

            def normalise(b):
                dve.wait_ge(rstd_ready, b + 1)
                dve.wait_ge(moments1, TB * (b + 1))
                if b >= 2:
                    dve.wait_ge(xnT_psum, b - 1)
                for j in range(TB):
                    t = TB * b + j
                    V.tensor_scalar(xn[:, b % 2, j, :], x[:, t, :], mv[:, t, 0:1], rstd[:, t:t + 1],
                                    ALU.subtract, ALU.mult).then_inc(xn_ready, 1)

            dve.wait_ge(small_in, 16)
            link(V.tensor_tensor(wq, wq, raw_wq[:, :, 1, :], ALU.add))
            link(V.tensor_tensor(wq, wq, raw_wq[:, :, 2, :], ALU.add))
            V.tensor_tensor(wq, wq, raw_wq[:, :, 3, :], ALU.add).then_inc(wq_summed, 1)
            dve.wait_ge(x_in[0], 16)
            moments(0, mv, moments1)
            dve.wait_ge(const_in, 16)

            def rope_keys(g):
                dve.wait_ge(k_psum, g + 1)
                kr = krot[:, 4 * g:4 * g + 4, :]
                both = lambda n: c(n).rearrange("p (o a) -> p o a", o=1).broadcast_to([P, 4, A])
                V.tensor_tensor(kr, bank[2 + 2 * g][:, 0:4 * A].rearrange("p (b a) -> p b a", b=4), both("kcos"),
                                ALU.mult).then_inc(dve_step, 1)
                V.tensor_tensor(ktmp[:, :, :], bank[3 + 2 * g][:, 0:4 * A].rearrange("p (b a) -> p b a", b=4),
                                both("ksin"), ALU.mult).then_inc(dve_step, 1)
                n_step[0] += 2
                settle()
                V.tensor_tensor(kr, kr, ktmp[:, :, :], ALU.add).then_inc(krot_ready, 1)

            rope_keys(0)
            normalise(0)
            dve.wait_ge(x_in[1], 16)
            moments(1, mv, moments1)
            dve.wait_ge(krot_ready, 1)
            rope_keys(1)
            link(V.tensor_copy(before_bf[:, :], c("before")))
            dve.wait_ge(tanh_ready, 1)
            link(V.tensor_scalar(tg[:, 0:1], tg[:, 0:1], 1.0 / KVH, None, ALU.mult))
            def normalise2(b):
                dve.wait_ge(rstd2_ready, b + 1)
                dve.wait_ge(moments2, TB * (b + 1))
                if b >= 1:
                    dve.wait_ge(xn2T_psum, b)
                    dve.wait_ge(xn2_out, 16 * b)
                for j in range(TB):
                    t = TB * b + j
                    V.tensor_scalar(xn2[:, j, :], x[:, t, :], mv2[:, t, 0:1], rstd2[:, t:t + 1],
                                    ALU.subtract, ALU.mult).then_inc(xn2_ready, 1)

            def rotate_q(b):
                dve.wait_ge(q_psum, b + 1)
                if b >= 1:
                    dve.wait_ge(s_psum, TB * b)
                V.tensor_tensor(qrot[:, :], bank[1][:, 0:S], c("rope"), ALU.mult).then_inc(qrot_ready, 1)

            def normalise_probs(b, j):
                dve.wait_ge(exp_done, KVH * (TB * b + j + 1))
                link(V.reciprocal(den[:, j, :], den[:, j, :]))
                V.tensor_tensor(probs[:, j, :, :], probs[:, j, :, :],
                                den[:, j, :].rearrange("p (h o) -> p h o", o=1).broadcast_to([P, KVH, A]),
                                ALU.mult).then_inc(probs_ready, 1)

            dve.wait_ge(x_in[2], 16)
            moments(2, mv, moments1)
            rotate_q(0)
            normalise(1)
            for t in range(B + 3):
                if t < B:
                    for j in range(TB):
                        dve.wait_ge(s_psum, TB * t + j + 1)
                        link(V.tensor_reduce(negmax[:, j, :],
                                             bank[2 + j][:, 0:KVH * A].rearrange("p (h a) -> p h a", h=KVH),
                                             AX.X, ALU.max))
                        V.tensor_scalar(negmax[:, j, :], negmax[:, j, :], -(HD ** -0.5), None,
                                        ALU.mult).then_inc(negmax_ready, 1)
                if 2 <= t < B + 2:
                    normalise2(t - 2)
                if t + 3 < B:
                    dve.wait_ge(x_in[t + 3], 16)
                    moments(t + 3, mv, moments1)
                if t + 1 < B:
                    rotate_q(t + 1)
                if t < B:
                    normalise_probs(t, 0)
                    normalise_probs(t, 1)
                if 1 <= t <= B:
                    b = t - 1
                    dve.wait_ge(att_psum, b + 1)
                    for j in range(TB):
                        tt = TB * b + j
                        V.scalar_tensor_tensor(out=x[:, tt, :], in0=bank[7][:, j * D:(j + 1) * D], scalar=tg[:, 0:1],
                                               in1=x[:, tt, :], op0=ALU.mult, op1=ALU.add).then_inc(x2_ready, 1)
                if t < B:
                    dve.wait_ge(pT_psum, 2 * t + 2)
                    if t >= 1:
                        dve.wait_ge(o_psum, t)
                    V.tensor_copy(probsT[:, 2:4, :].rearrange("a h s -> a (h s)"), bank[5][0:A, :])\
                     .then_inc(pT_dve, 1)
                if 1 <= t <= B:
                    dve.wait_ge(x2_ready, TB * t)
                    moments(t - 1, mv2, moments2)
                if t + 2 < B:
                    normalise(t + 2)
                if t >= 3:
                    b = t - 3
                    dve.wait_ge(lg_psum, b + 1)
                    V.tensor_copy(logits[:, TB * b:TB * b + TB, :].rearrange("p t e -> p (t e)"),
                                  bank[6][:, S:S + TB * E]).then_inc(lg_ready, 1)

            dve.wait_ge(lg_ready, B)
            per_tile = lambda ap: ap.rearrange("p (t o) -> p t o", o=1).broadcast_to([P, NT, E])
            per_expert = lambda ap: ap.rearrange("p (o e) -> p o e", o=1).broadcast_to([P, NT, E])
            link(V.tensor_reduce(pscore[:, :], logits[:, :, :], AX.X, ALU.max))
            V.tensor_tensor(rb[:, :, :], logits[:, :, :], per_tile(pscore[:, :]), ALU.subtract).then_inc(shifted, 1)
            dve.wait_ge(rexp_ready, 1)
            for k in range(2):
                src = rexp if k == 0 else ra
                link(V.tensor_reduce(pmax[:, k, :], src[:, :, :], AX.X, ALU.max))
                link(V.tensor_tensor(rb[:, :, :], src[:, :, :], per_tile(pmax[:, k, :]), ALU.is_equal))
                link(V.tensor_tensor(rb[:, :, :], rb[:, :, :], per_expert(c("prio")), ALU.mult))
                link(V.tensor_reduce(pscore[:, :], rb[:, :, :], AX.X, ALU.max))
                link(V.tensor_tensor(pick[:, k, :, :], rb[:, :, :], per_tile(pscore[:, :]), ALU.is_equal))
                if k == 0:
                    link(V.scalar_tensor_tensor(out=ra[:, :, :], in0=pick[:, 0, :, :], scalar=-4.0,
                                                in1=rexp[:, :, :], op0=ALU.mult, op1=ALU.add))
            V.memset(chosen[:, NT:NT + 1, :], 0.0).then_inc(chosen_ready, 1)
            V.tensor_tensor(chosen[:, 0:NT, :], pick[:, 0, :, :], pick[:, 1, :, :], ALU.add).then_inc(chosen_ready, 3)
            link(V.tensor_tensor(pscore[:, :], pmax[:, 0, :], pmax[:, 1, :], ALU.add))
            link(V.reciprocal(pscore[:, :], pscore[:, :]))
            link(V.tensor_scalar(pscore[:, :], pscore[:, :], tg[:, 1:2], None, ALU.mult))
            for k in range(2):
                link(V.tensor_tensor(pmax[:, k, :], pmax[:, k, :], pscore[:, :], ALU.mult))
            w_flat = pmax[:, :, :].rearrange("p k t -> p (k t)")
            whi_r = hT[:, 0, 0, 0:2 * NT]
            link(V.tensor_copy(whi_r, w_flat))
            link(V.tensor_copy(wparts[:, 0, :], whi_r))
            link(V.tensor_tensor(wparts[:, 1, :], w_flat, wparts[:, 0, :], ALU.subtract))
            dve.wait_ge(rank_psum, 1)
            link(V.tensor_copy(slotpos[:, :, :].rearrange("p t e -> p (t e)"), bank[0][:, 0:(NT + 1) * E]))
            for k in range(2):
                link(V.tensor_tensor(rb[:, :, :], pick[:, k, :, :], slotpos[:, 0:NT, :], ALU.mult))
                link(V.tensor_reduce(rank[:, k * NT:(k + 1) * NT], rb[:, :, :], AX.X, ALU.add))
            link(V.tensor_copy(rank_i[:, 0, :], rank[:, :]))
            link(V.tensor_scalar(rank_i[:, 1, :], rank_i[:, 0, :], P - 1, None, ALU.bitwise_and))
            V.tensor_copy(slot_f[:, 1, :], rank_i[:, 1, :]).then_inc(row_ready, 1)
            link(V.tensor_scalar(rank_i[:, 0, :], rank_i[:, 0, :], 7, None, ALU.arith_shift_right))
            link(V.tensor_copy(slot_f[:, 0, :], rank_i[:, 0, :]))
            cmp_ = rcmp[:, 0:E * 15].rearrange("p (e n) -> p e n", e=E)
            link(V.tensor_tensor(cmp_, slotpos[:, NT, :].rearrange("p (e o) -> p e o", o=1).broadcast_to([P, E, 15]),
                                 c("steps").rearrange("p (o n) -> p o n", o=1).broadcast_to([P, E, 15]), ALU.is_gt))
            link(V.tensor_reduce(nblk[:, :], cmp_, AX.X, ALU.add))
            link(V.tensor_scalar(nblk[:, :], nblk[:, :], 1.0, None, ALU.add))
            cum = rcmp[:, 0:E * E].rearrange("p (e n) -> p e n", e=E)
            link(V.tensor_tensor(cum, c("upto").rearrange("p (e n) -> p e n", e=E),
                                 nblk[:, :].rearrange("p (o e) -> p o e", o=1).broadcast_to([P, E, E]), ALU.mult))
            link(V.tensor_reduce(endblk[:, :], cum, AX.X, ALU.add))
            link(V.tensor_tensor(startblk[:, :], endblk[:, :], nblk[:, :], ALU.subtract))
            for k in range(2):
                link(V.tensor_tensor(rb[:, :, :], pick[:, k, :, :], per_expert(startblk[:, :]), ALU.mult))
                link(V.tensor_reduce(rank[:, k * NT:(k + 1) * NT], rb[:, :, :], AX.X, ALU.add))
            link(V.tensor_tensor(slot_f[:, 0, :], slot_f[:, 0, :], rank[:, :], ALU.add))
            oh = rcmp.rearrange("p (n s) -> p n s", n=2 * NT)
            per_slot = lambda ap: ap.rearrange("p (n o) -> p n o", o=1).broadcast_to([P, 2 * NT, NCOL])
            V.tensor_tensor(oh, per_slot(slot_f[:, 0, :]),
                            c("blocks").rearrange("p (o s) -> p o s", o=1).broadcast_to([P, 2 * NT, NCOL]),
                            ALU.is_equal).then_inc(oh_block, 1)
            for g in range(n_oh // 8):
                V.tensor_tensor(oh_hT[:, 8 * g:8 * g + 8, :] if g < 2 else oh_more[:, :, :],
                                c("iota").rearrange("p (o q) -> p o q", o=1).broadcast_to([P, 8, P]),
                                slot_f[:, 1, 8 * g:8 * g + 8].rearrange("p (n o) -> p n o", o=1)
                                .broadcast_to([P, 8, P]), ALU.is_equal).then_inc(onehot_ready, 1)
            dve.wait_ge(oh_block, 1)
            for q in range(2):
                V.tensor_tensor(spread[:, :, 1 + q, :], oh, per_slot(wparts[:, q, :]), ALU.mult).then_inc(spread_tok, 1)
            by_block = table_area[:, 0:NCOL * E].rearrange("p (s e) -> p s e", e=E)
            all_blocks = c("blocks").rearrange("p (s o) -> p s o", o=1).broadcast_to([P, NCOL, E])
            for_blocks = lambda ap: ap.rearrange("p (o e) -> p o e", o=1).broadcast_to([P, NCOL, E])
            link(V.tensor_tensor(by_block, for_blocks(endblk[:, :]), all_blocks, ALU.is_le))
            link(V.tensor_reduce(tabf[:, 0, :], by_block, AX.X, ALU.add))
            link(V.tensor_scalar(tabf[:, 0, :], tabf[:, 0, :], float(E - 1), None, ALU.min))
            link(V.tensor_copy(tab[:, 0, :], tabf[:, 0, :]))
            dve.wait_ge(onehot_used, 2 * NT)
            link(V.tensor_copy(idxf[:, 0, :], bank[1][:, 0:NCOL]))
            link(V.tensor_scalar(idxf[:, 1, :], idxf[:, 0, :], 0.0, None, ALU.is_equal))
            link(V.tensor_scalar(idxf[:, 1, :], idxf[:, 1, :], c("spare"), -1.0, ALU.mult, ALU.add))
            link(V.tensor_tensor(idxf[:, 0, :], idxf[:, 0, :], idxf[:, 1, :], ALU.add))
            V.tensor_copy(idx[:, :], idxf[:, 0, :]).then_inc(idx_ready, 1)
            link(V.tensor_copy(wslot[:, :], bank[1][:, NCOL:2 * NCOL]))
            link(V.tensor_tensor(wslot[:, :], wslot[:, :], bank[1][:, 2 * NCOL:3 * NCOL], ALU.add))
            link(V.tensor_scalar(endblk[:, :], endblk[:, :], -1.0, None, ALU.add))
            for p in range(3):
                link(V.tensor_tensor(nblk[:, :], startblk[:, :], endblk[:, :], ALU.min))
                link(V.tensor_tensor(by_block, for_blocks(nblk[:, :]), all_blocks, ALU.is_equal))
                link(V.tensor_tensor(by_block, by_block, for_blocks(c("follow")), ALU.mult))
                link(V.tensor_reduce(tabf[:, p + 1, :], by_block, AX.X, ALU.add))
                link(V.tensor_scalar(startblk[:, :], startblk[:, :], 1.0, None, ALU.add))
            V.tensor_copy(tab[:, 1:4, :], tabf[:, 1:4, :]).then_inc(tables_ready, 1)

            def x_low(s, par):
                dve.wait_ge(xT_hi, s + 1)
                V.tensor_tensor(xT[:, par, 1, :, :].rearrange("p c t -> p (c t)"), bank[7][:, 0:D],
                                xT[:, par, 0, :, :].rearrange("p c t -> p (c t)"), ALU.subtract).then_inc(xT_split, 1)

            def product(s, hf):
                dve.wait_ge(silu_made, 2 * s + hf + 1)
                if not isinstance(s, int) or s >= 1:
                    dve.wait_ge(hT_made, 2 * s + hf - 1)
                V.tensor_tensor(h[:, hf, :], silu[:, hf, :], bank[2 * hf + 1][:, :], ALU.mult).then_inc(h_made, 1)

            def h_low(s, hf):
                dve.wait_ge(hT_hi, 2 * s + hf + 1)
                V.tensor_tensor(hT[:, hf, 1, :], bank[4 + hf][:, :], hT[:, hf, 0, :], ALU.subtract)\
                 .then_inc(hT_split, 1)

            def weigh(s):
                dve.wait_ge(y_made, s + 1)
                dve.wait_ge(y_free, s + 1)
                V.tensor_scalar(y[:, :, :].rearrange("p r d -> p (r d)")[:, bass.ds((s & (RING - 1)) * D, D)],
                                bank[6][:, 0:D], wslot[:, bass.ds(s, 1)], None, ALU.mult).then_inc(y_out, 1)

            def step(s, par, first=False, ahead=1):
                product(s, 0)
                if not first:
                    h_low(s - 1, 1)
                if ahead:
                    x_low(s + 1, 1 - par)
                product(s, 1)
                h_low(s, 0)
                if not first:
                    weigh(s - 1)

            x_low(0, 0)
            step(0, 0, first=True)
            with dve.Fori(0, (NBLK - 3) // 2) as i:
                step(i * 2 + 1, 1)
                step(i * 2 + 2, 0)
            step(NBLK - 2, 1)
            step(NBLK - 1, 0, ahead=0)
            h_low(NBLK - 1, 1)
            weigh(NBLK - 1)


def shape_constants():
    out = np.zeros((P, NCONST), np.float32)

    def put(name, value):
        a, b = CONSTS[name]
        out[:, a:b] = value

    inv = (np.float32(1.0) / np.float32(10000.0) ** (np.arange(0, HD, 2, dtype=np.float32) / np.float32(HD)))
    ang = np.arange(S, dtype=np.float32)[:, None] * inv[None, :].astype(np.float32)
    cos, sin = np.cos(ang).astype(np.float32), np.sin(ang).astype(np.float32)
    row = np.arange(P) % HR
    d = row % HD
    sign = np.where(d % 2 == 0, -1.0, 1.0).astype(np.float32)[:, None]
    put("ident", np.eye(P))
    put("rope", np.where((row < HD)[:, None], cos[:, d // 2].T, sign * sin[:, d // 2].T))
    put("kcos", cos[:A, d // 2].T)
    put("ksin", sign * sin[:A, d // 2].T)
    put("headmask", np.repeat((np.arange(P)[:, None] // HR == np.arange(KVH)[None, :]), A, axis=1))
    put("before", np.arange(P)[:, None] < np.arange(P)[None, :])
    put("iota", np.arange(P)[None, :])
    put("prio", E - np.arange(E)[None, :])
    put("steps", P * np.arange(1, 16)[None, :])
    put("upto", (np.arange(E)[None, :] <= np.arange(E)[:, None]).reshape(1, E * E))
    put("blocks", np.arange(NCOL)[None, :])
    put("token1", np.arange(NT)[None, :] * P + np.arange(P)[:, None] + 1)
    put("follow", np.where((np.arange(E) >= 1) & (np.arange(E) <= E - 2), np.arange(E), 0)[None, :])
    put("spare", np.arange(P)[:, None] + T + 1)
    return out


def kernel(**inputs):
    import concourse.bacc as bacc
    from concourse.bass_utils import run_bass_kernel_spmd

    x = np.ascontiguousarray(inputs["x"]).reshape(T, D)
    ctx = np.ascontiguousarray(inputs["ctx_1024"])
    Wq, Wk, Wv, Wo = (np.ascontiguousarray(inputs[f"L0_xattn_{n}"]) for n in ("Wq", "Wk", "Wv", "Wo"))
    gate = np.ascontiguousarray(inputs["L0_ffn_gate_w"])
    gup = np.ascontiguousarray(inputs["L0_ffn_gate_up_proj"])
    down = np.ascontiguousarray(inputs["L0_ffn_down_proj"])
    g2 = np.concatenate([np.ascontiguousarray(inputs["g_xattn"]), np.ascontiguousarray(inputs["g_ffn"])])

    swap = np.arange(HD) ^ 1

    def by_chunk(a):
        return a.reshape(KC, P, -1).transpose(1, 0, 2).reshape(P, -1)

    q4 = Wq.reshape(D, KVH, GROUPS, HD).transpose(0, 2, 1, 3)
    q4 = np.concatenate([q4, q4[..., swap]], axis=-1).reshape(D, -1)
    ka = np.concatenate([Wk, Wk], axis=-1).reshape(D, -1)
    kb = np.concatenate([Wk[..., swap], Wk[..., swap]], axis=-1).reshape(D, -1)
    small = np.concatenate([by_chunk(q4), by_chunk(ka), by_chunk(kb), by_chunk(Wv.reshape(D, -1)),
                            by_chunk(gate.T), np.broadcast_to(g2[None, :], (P, 2))], axis=1)
    arrays = {
        "x": x,
        "ctxT": ctx.reshape(B * A, KC, P).transpose(2, 1, 0),
        "small": small,
        "wo": Wo,
        "gu": gup.transpose(0, 2, 1).reshape(E, KC, P, 2 * I).transpose(0, 2, 1, 3).reshape(E, P, GU),
        "dn": down.transpose(0, 2, 1).reshape(E, I // P, P, D).transpose(0, 2, 1, 3).reshape(E, P, DN),
        "consts": shape_constants(),
    }
    arrays = {k: np.ascontiguousarray(a) for k, a in arrays.items()}
    nc = bacc.Bacc("TRN2", target_bir_lowering=False, num_devices=1)
    aps = [nc.dram_tensor(f"in_{k}", a.shape, mybir.dt.from_np(a.dtype), kind="ExternalInput").ap() for k, a in arrays.items()]
    out = nc.dram_tensor("out", (T + P, D), F32, kind="ExternalOutput").ap()
    build_program(nc, *aps, out)
    r = run_bass_kernel_spmd(nc, [{f"in_{k}": a for k, a in arrays.items()}], core_ids=[0])
    return r.results[0]["out"][:T].reshape(B, S, D)
```

```python
from contextlib import ExitStack

import numpy as np
import concourse.bass as bass
from concourse import mybir

F32 = mybir.dt.float32
F32R = mybir.dt.float32r
BF16 = mybir.dt.bfloat16
I32 = mybir.dt.int32
ALU = mybir.AluOpType
ACT = mybir.ActivationFunctionType
AX = mybir.AxisListType

P = 128
B, S, D = 8, 256, 256
A = 120
KVH, GROUPS, HD = 4, 4, 16
E, I = 8, 1024
T = B * S
NT = T // P
TB = S // P
KC = D // P
HR = 2 * HD
EPS = 1e-5
NBLK = (2 * T + E * (P - 1)) // P
NCOL = NBLK + 3
FULL = 2 * T // P
XW = D + E
PAIRS = (FULL - 1) // 2
HALF = I // 2
JH = HALF // P
GU = KC * 2 * I
DN = (I // P) * D
RING = 4
CODES = 8 * (E - 2) + 7
PIECE = GU // 2
assert DN == PIECE

CONSTS = {}


def _const_columns():
    at = 0
    for name, n in (("ident", P), ("rope", S), ("kcos", A), ("ksin", A), ("headmask", KVH * A),
                    ("before", P), ("iota", P), ("prio", E), ("steps", T // P), ("earlier", E * E),
                    ("blocks", NCOL), ("token1", NT), ("spare", 1), ("first", E), ("alone", E), ("second", E)):
        CONSTS[name] = (at, at + n)
        at += n
    return at


NCONST = _const_columns()
KPART = 2 * KC * P + KC * KVH * HD + KC * E + 2
NSMALL = KPART + KC * GROUPS * P


def build_program(nc, x_d, ctx_d, small_d, wo_d, gu_d, dn_d, const_d, out_d):
    xn2_d = nc.dram_tensor("xn2_scratch", (T + P, XW), F32, kind="Internal").ap()
    ctx = ExitStack()
    with ctx:
        def sb(name, shape, dt=F32):
            return ctx.enter_context(nc.sbuf_tensor(name, shape, dt))

        def sem(name):
            return ctx.enter_context(nc.semaphore(name))

        x = sb("x", [P, NT, D])
        const = sb("const", [P, NCONST])
        small = sb("small", [P, NSMALL])
        wka, wkb, wv, gw, gates = (small[:, a:b] for a, b in ((0, 256), (256, 512), (512, 640), (640, 656), (656, 658)))
        raw_wq = small[:, KPART:NSMALL].rearrange("p (c g n) -> p c g n", c=KC, g=GROUPS)
        wq = raw_wq[:, :, 0, :]
        wo = sb("wo", [HD, D])
        area = sb("area", [P, 3840 + KVH * S])
        ctxT = area[:, 0:KC * B * A].rearrange("p (k n) -> p k n", k=KC)
        krot = area[:, 1920:1920 + B * A].rearrange("p (b a) -> p b a", b=B)
        kbd = area[:, 2880:2880 + 2 * KVH * A].rearrange("p (q h a) -> p q h a", q=2, h=KVH)
        count_area = area[:, 0:E * (T // P)]
        oh_blocks = area[:, 0:2 * NT * NCOL]
        table_area = area[:, 2 * NT * NCOL:3840]
        v = sb("v", [A, B * KVH * HD])
        stats = sb("stats", [P, NT, 6])
        mv = sb("mv", [P, NT, 2])
        mv2 = sb("mv2", [P, NT, 2])
        rstd = sb("rstd", [P, NT])
        rstd2 = sb("rstd2", [P, NT])
        vareps = sb("vareps", [P, 2, TB])
        expo = sb("expo", [P, 1])
        xn = sb("xn", [P, 2, TB, D])
        xnT = sb("xnT", [P, KC, S])
        qrot = sb("qrot", [P, S])
        probs = sb("probs", [P, TB, KVH, A])
        negmax = sb("negmax", [P, TB, KVH])
        den = sb("den", [P, TB, KVH])
        probsT = area[0:A, 3840:3840 + KVH * S].rearrange("a (h s) -> a h s", h=KVH)
        oT = sb("oT", [HD, S])
        xn2 = sb("xn2", [P, TB, D])
        ktmp = xn2[:, :, :].rearrange("p t d -> p (t d)")[:, 0:4 * A].rearrange("p (b a) -> p b a", b=4)
        xn2T = sb("xn2T", [P, KC, S])
        tg = sb("tg", [P, 2])
        zrow = xn2T[:, 0, :]
        logits = sb("logits", [P, NT, E])
        rwork = small[:, KPART:KPART + 8 * NT * E]
        ra, rb, rexp = (rwork[:, n * NT * E:(n + 1) * NT * E].rearrange("p (t e) -> p t e", e=E) for n in range(3))
        pick, prod = (rwork[:, n * NT * E:(n + 2) * NT * E].rearrange("p (k t e) -> p k t e", k=2, e=E) for n in (3, 5))
        wdense = rwork[:, 7 * NT * E:].rearrange("p (t e) -> p t e", e=E)
        slotpos = rb
        pmax = sb("pmax", [P, 2, NT])
        pscore = sb("pscore", [P, NT])
        chosen = sb("chosen", [P, NT + 1, E], BF16)
        before_bf = sb("before_bf", [P, P], BF16)
        ones_bf = sb("ones_bf", [P, P], BF16)
        nblk = sb("nblk", [P, E])
        endblk = sb("endblk", [P, E])
        rank = sb("rank", [P, 2 * NT])
        rank_i = sb("rank_i", [P, 2, 2 * NT], I32)
        slot_f = sb("slot_f", [P, 2, 2 * NT])
        by_piece = table_area[:, 0:2 * NCOL * E].rearrange("p (n s e) -> p n s e", n=2, e=E)
        by_block = by_piece[:, 0, :, :]
        tabf = table_area[:, 2 * NCOL * E:2 * NCOL * E + 4 * NCOL].rearrange("p (n s) -> p n s", n=4)
        slotT = table_area[0:NCOL, 2 * NCOL * E + 4 * NCOL:2 * NCOL * E + 4 * NCOL + P]
        empty = table_area[:, 2 * NCOL * E + 4 * NCOL + P:2 * NCOL * E + 5 * NCOL + P]
        piece_at = sb("piece_at", [P, 2, E])
        piece_code = sb("piece_code", [P, 2, E])
        idx = sb("idx", [P, NCOL], I32)
        startblk = sb("startblk", [P, E])
        tab = sb("tab", [P, 4, NCOL], I32)
        last_block = sb("last_block", [P, 1], I32)
        idx_g = sb("idx_g", [P, 1], I32)
        idx_s = sb("idx_s", [P, 1], I32)
        wraw = sb("wraw", [P, GU + DN])
        gu = sb("gu", [P, 2, 2, GU], F32R)
        dn = sb("dn", [P, 2, 2, DN], F32R)
        late = x[:, :, :].rearrange("p t d -> p (t d)")
        xg_flat = small[:, 0:RING * XW]
        y = late[:, RING * D:2 * RING * D].rearrange("p (r d) -> p r d", r=RING)
        silu = late[:, 2 * RING * D:2 * RING * D + I].rearrange("p (q n) -> p q n", q=2)
        h = late[:, 2 * RING * D + I:2 * RING * D + 2 * I].rearrange("p (q n) -> p q n", q=2)
        weights = late[:, 0:8 * E]
        xs = xn[:, 0, 0, :]
        xT = sb("xT", [P, 2, 2, KC, P], F32R)
        hT = sb("hT", [P, 2, 2, JH * P], F32R)
        oh_dve = hT[:, :, :, :].rearrange("p a b (n q) -> p (a b n) q", q=P)
        oh_pool = xT[:, :, :, :, :].rearrange("p a b c q -> p (a b c) q")
        marked = sb("marked", [P, 2, NT, NCOL], F32R)
        bank = [ctx.enter_context(nc.psum_tensor(f"bank{i}", [P, 512], F32)) for i in range(8)]

        def c(name, n=P):
            a, b = CONSTS[name]
            return const[0:n, a:b]

        ident = c("ident")

        zero_xe, masks_in = sem("zero_xe"), sem("masks_in")
        const_in, wkv_in, wq_in, wo_in = (sem(n) for n in ("const_in", "wkv_in", "wq_in", "wo_in"))
        ctx_in = [sem(f"ctx_in{g}") for g in range(2)]
        x_in = [sem(f"x_in{b}") for b in range(B)]
        dve_step, pool_step = sem("dve_step"), sem("pool_step")
        wq_summed, k_psum, krot_ready, kbd_ready, v_psum, v_ready, tanh_ready = (
            sem(n) for n in ("wq_summed", "k_psum", "krot_ready", "kbd_ready", "v_psum", "v_ready", "tanh_ready"))
        xn_ready, xnT_psum, xnT_ready, q_psum, qrot_ready, s_psum, negmax_ready, exp_done, probs_ready = (
            sem(n) for n in ("xn_ready", "xnT_psum", "xnT_ready", "q_psum", "qrot_ready", "s_psum",
                             "negmax_ready", "exp_done", "probs_ready"))
        pT_psum, pT_copied, o_psum, oT_ready, att_psum, x2_ready = (
            sem(n) for n in ("pT_psum", "pT_copied", "o_psum", "oT_ready", "att_psum", "x2_ready"))
        xn2_ready, xn2T_psum, xn2T_ready, lg_psum, lg_ready = (
            sem(n) for n in ("xn2_ready", "xn2T_psum", "xn2T_ready", "lg_psum", "lg_ready"))
        out_init, xn2_out, zrow_ready, zero_xn2, zero_out = (
            sem(n) for n in ("out_init", "xn2_out", "zrow_ready", "zero_xn2", "zero_out"))
        shifted, rexp_ready, chosen_ready, rank_psum, onehot_ready, onehot_used, slots_psum, tables_ready = (
            sem(n) for n in ("shifted", "rexp_ready", "chosen_ready", "rank_psum", "onehot_ready", "onehot_used",
                             "slots_psum", "tables_ready"))
        w_in = [sem(f"w_in{p}") for p in range(3)]
        w_hi, w_lo = sem("w_hi"), sem("w_lo")
        moments1, moments2, rstd_ready, rstd2_ready, oh_block, idx_ready = (
            sem(n) for n in ("moments1", "moments2", "rstd_ready", "rstd2_ready", "oh_block", "idx_ready"))
        row_ready = sem("row_ready")
        wdense_ready, wdense_out, onehot_pool, marked_ready, slotT_ready, experts_ready, all_landed = (
            sem(n) for n in ("wdense_ready", "wdense_out", "onehot_pool", "marked_ready", "slotT_ready",
                             "experts_ready", "all_landed"))
        index_settled, weights_kept = sem("index_settled"), sem("weights_kept")
        idx_g_ready, idx_s_ready, x_gathered, y_added, y_free = (
            sem(n) for n in ("idx_g_ready", "idx_s_ready", "x_gathered", "y_added", "y_free"))
        x_staged, xT_made, xT_hi, xT_split = (sem(n) for n in ("x_staged", "xT_made", "xT_hi", "xT_split"))
        gu_made, silu_made, h_made, hT_made, hT_hi, hT_split, y_made, y_out = (
            sem(n) for n in ("gu_made", "silu_made", "h_made", "hT_made", "hT_hi", "hT_split", "y_made", "y_out"))

        block = ctx.enter_context(nc.Block())

        def gu_part(where, part, col, n):
            flat = gu[:, :, :, :].rearrange("p s q n -> p (s q n)")
            return flat[:, bass.ds(where * (2 * GU) + (part * GU + col), n)]

        def dn_part(where, part, col, n):
            flat = dn[:, :, :, :].rearrange("p s q n -> p (s q n)")
            return flat[:, bass.ds(where * (2 * DN) + (part * DN + col), n)]

        def piece_of(where, part, p):
            return gu_part(where, part, p * PIECE, PIECE) if p < 2 else dn_part(where, part, 0, DN)

        @block.sync
        def _(sp):
            HB = 4 * A
            sp.dma_start(small[:, 0:KPART], small_d[:, 0:KPART]).then_inc(wkv_in, 16)
            sp.dma_start(ctxT[:, :, 0:HB], ctx_d[:, :, 0:HB]).then_inc(ctx_in[0], 16)
            x_v = x_d.rearrange("(t p) d -> p t d", p=P)
            sp.dma_start(x[:, 0:TB, :], x_v[:, 0:TB, :]).then_inc(x_in[0], 16)
            EARLY_CONST = CONSTS["headmask"][0]
            sp.dma_start(const[:, 0:EARLY_CONST], const_d[:, 0:EARLY_CONST]).then_inc(const_in, 16)
            sp.dma_start(raw_wq, small_d[:, KPART:NSMALL].rearrange("p (c g n) -> p c g n", c=KC, g=GROUPS))\
              .then_inc(wq_in, 16)
            sp.dma_start(const[:, EARLY_CONST:NCONST], const_d[:, EARLY_CONST:NCONST]).then_inc(masks_in, 16)
            sp.dma_start(ctxT[:, :, HB:2 * HB], ctx_d[:, :, HB:2 * HB]).then_inc(ctx_in[1], 16)
            for b in range(1, B):
                sp.dma_start(x[:, TB * b:TB * b + TB, :], x_v[:, TB * b:TB * b + TB, :]).then_inc(x_in[b], 16)
            sp.dma_start(wo[:, :], wo_d).then_inc(wo_in, 16)

            def load_piece(q):
                e, p = divmod(q, 3)
                if e >= 1:
                    sp.wait_ge(w_lo, q - 2)
                src = gu_d[e][:, p * PIECE:(p + 1) * PIECE] if p < 2 else dn_d[e]
                sp.dma_start(wraw[:, p * PIECE:(p + 1) * PIECE], src).then_inc(w_in[p], 16)

            for q in range(3):
                load_piece(q)
            sp.wait_ge(zrow_ready, 1)
            sp.dma_start(out_d[T:T + P, :], zrow).then_inc(zero_out, 16)
            sp.dma_start(xn2_d[T:T + P, 0:D], zrow).then_inc(zero_xn2, 16)
            sp.dma_start(xn2_d[T:T + P, D:XW], zrow[:, 0:E]).then_inc(zero_xe, 16)
            out_v = out_d[0:T, :].rearrange("(t p) d -> p t d", p=P)
            xn2_v = xn2_d[0:T, 0:D].rearrange("(t p) d -> p t d", p=P)
            for b in range(B):
                sp.wait_ge(x2_ready, TB * (b + 1))
                sp.dma_start(out_v[:, TB * b:TB * b + TB, :], x[:, TB * b:TB * b + TB, :]).then_inc(out_init, 16)
                sp.wait_ge(xn2_ready, TB * (b + 1))
                sp.dma_start(xn2_v[:, TB * b:TB * b + TB, :], xn2[:, :, :]).then_inc(xn2_out, 16)
                if 1 <= b <= 3:
                    load_piece(b + 2)
            sp.wait_ge(wdense_ready, 1)
            sp.dma_start(xn2_d[0:T, D:XW].rearrange("(t p) e -> p t e", p=P), wdense[:, :, :]).then_inc(wdense_out, 16)
            for q in range(6, 3 * E):
                load_piece(q)
            sp.wait_ge(out_init, 16 * B)
            sp.wait_ge(zero_out, 16)
            sp.wait_ge(all_landed, 1)

        @block.gpsimd
        def _(pool):
            nc.gpsimd.memset(ones_bf[:, :], 1.0).then_inc(pool_step, 1)
            nc.gpsimd.memset(zrow, 0.0).then_inc(zrow_ready, 1)
            nc.gpsimd.memset(expo[:, :], -0.5).then_inc(zrow_ready, 1)
            pool.sem_inc(y_free, RING)

            def split_low(e, p):
                pool.wait_ge(w_hi, 3 * e + (p + 1))
                where = e & 1
                nc.gpsimd.tensor_tensor(piece_of(where, 1, p), wraw[:, p * PIECE:(p + 1) * PIECE],
                                        piece_of(where, 0, p), ALU.subtract).then_inc(w_lo, 1)

            n_step = [1]

            def rsqrt(done, b, var, out, sig):
                pool.wait_ge(done, TB * (b + 1))
                n_step[0] += 1
                tmp = vareps[:, n_step[0] % 2, :]
                nc.gpsimd.tensor_scalar(tmp, var[:, TB * b:TB * b + TB, 1], EPS, None, ALU.add).then_inc(pool_step, 1)
                pool.wait_ge(pool_step, n_step[0])
                nc.gpsimd.tensor_tensor(out[:, TB * b:TB * b + TB], tmp, expo[:, 0:1].broadcast_to([P, TB]),
                                        ALU.pow).then_inc(sig, 1)
                pool.wait_ge(sig, b + 1)

            def spread_keys(b):
                pool.wait_ge(krot_ready, b // 4 + 1)
                if b >= 2:
                    pool.wait_ge(s_psum, TB * (b - 1))
                mask = c("headmask").rearrange("p (h a) -> p h a", h=KVH)
                nc.gpsimd.tensor_tensor(kbd[:, b % 2, :, :],
                                        krot[:, b, :].rearrange("p (o a) -> p o a", o=1).broadcast_to([P, KVH, A]),
                                        mask, ALU.mult).then_inc(kbd_ready, 1)

            pool.wait_ge(zrow_ready, 2)
            rsqrt(moments1, 0, mv, rstd, rstd_ready)
            pool.wait_ge(masks_in, 16)
            spread_keys(0)
            rsqrt(moments1, 1, mv, rstd, rstd_ready)
            spread_keys(1)
            rsqrt(moments1, 2, mv, rstd, rstd_ready)
            for t in range(B + 1):
                if t >= 1:
                    rsqrt(moments2, t - 1, mv2, rstd2, rstd2_ready)
                if t + 3 < B:
                    rsqrt(moments1, t + 3, mv, rstd, rstd_ready)
                if t + 2 < B:
                    spread_keys(t + 2)
                if 1 <= t <= 4:
                    split_low(*divmod(t - 1, 3))
            split_low(1, 1)
            split_low(1, 2)
            pool.wait_ge(row_ready, 1)
            for m in range(8):
                t, k = NT - 4 + m // 2, m % 2
                nc.gpsimd.tensor_scalar(oh_pool[:, m, :], c("iota"), slot_f[:, 1, k * NT + t:k * NT + t + 1], None,
                                        ALU.is_equal).then_inc(onehot_pool, 1)

            def gather(g, r):
                nc.gpsimd.tensor_copy(idx_g[:, :], idx[:, bass.ds(g, 1)]).then_inc(idx_g_ready, 1)
                pool.wait_ge(idx_g_ready, g + 1)
                pool.sem_inc(index_settled, 1)
                nc.gpsimd.indirect_dma_start(
                    out=xg_flat[:, r * XW:(r + 1) * XW], out_offset=None, in_=xn2_d,
                    in_offset=bass.IndirectOffsetOnAxis(ap=idx_g[:, :], axis=0)).then_inc(x_gathered, 16)

            def scatter(n, r):
                pool.wait_ge(y_out, n + 1)
                nc.gpsimd.tensor_copy(idx_s[:, :], idx[:, bass.ds(n, 1)]).then_inc(idx_s_ready, 1)
                pool.wait_ge(idx_s_ready, n + 1)
                pool.sem_inc(index_settled, 1)
                nc.gpsimd.indirect_dma_start(
                    out=out_d, out_offset=bass.IndirectOffsetOnAxis(ap=idx_s[:, :], axis=0),
                    in_=y[:, r, :], in_offset=None, compute_op=ALU.add).then_inc(y_added, 16)

            def middle_piece(s):
                v = pool.value_load(tab[0:1, 1, bass.ds(s, 1)], min_val=0, max_val=CODES)
                with pool.If(v > 0):
                    split_low((v >> 3) + 1, 1)

            def end_pieces(s):
                v = pool.value_load(tab[0:1, 2, bass.ds(s, 1)], min_val=0, max_val=CODES)
                with pool.If(v > 0):
                    for p in range(3):
                        with pool.If((v & (1 << p)) > 0):
                            split_low((v >> 3) + 1, p)

            def step(s, r):
                pool.wait_ge(x_gathered, 16 * (s + 3))
                pool.wait_ge(weights_kept, s)
                gather(s + 3, r)
                middle_piece(s)
                scatter(s - 1, r)
                end_pieces(s)
                pool.wait_ge(y_added, 16 * s)
                pool.sem_inc(y_free, 1)

            pool.wait_ge(idx_ready, 1)
            pool.wait_ge(xn2_out, 16 * B)
            pool.wait_ge(wdense_out, 16)
            pool.wait_ge(zero_xn2, 16)
            pool.wait_ge(zero_xe, 16)
            pool.wait_ge(zero_out, 16)
            pool.wait_ge(out_init, 16 * B)
            for g in range(RING):
                if g >= 1:
                    pool.wait_ge(x_gathered, 16 * g)
                gather(g, g)
            pool.wait_ge(tables_ready, 1)
            SURE = (FULL - 1) // RING
            with pool.Fori(0, SURE) as i:
                for u in range(RING):
                    step(i * RING + (u + 1), u)

            def steps_while_used(s, r, n):
                used = pool.value_load(tab[0:1, 3, bass.ds(s, 1)], min_val=0, max_val=1)
                with pool.If(used > 0):
                    step(s, r)
                    if n > 1:
                        steps_while_used(s + 1, (r + 1) % RING, n - 1)

            ROUNDS = (NBLK - 1) // RING
            with pool.Fori(SURE, ROUNDS) as i:
                steps_while_used(i * RING + 1, 0, RING)
            steps_while_used(ROUNDS * RING + 1, 0, NBLK - 1 - ROUNDS * RING)
            last = pool.value_load(last_block[0:1, 0:1], min_val=FULL - 1, max_val=NBLK - 1)
            scatter(last, 0)
            pool.wait_ge(x_gathered, 16 * (last + RING))
            pool.wait_ge(y_added, 16 * (last + 1))
            pool.sem_inc(all_landed, 1)

        @block.scalar
        def _(act):
            act.wait_ge(wkv_in, 16)
            nc.scalar.activation(tg[:, :], gates, ACT.Tanh).then_inc(tanh_ready, 1)

            def split_high(e, p):
                act.wait_ge(w_in[p], (e + 1) * 16)
                where = e & 1
                nc.scalar.activation(piece_of(where, 0, p), wraw[:, p * PIECE:(p + 1) * PIECE],
                                     ACT.Copy).then_inc(w_hi, 1)

            EARLY = TB * (B - 3)

            def exp_logits(t0, t1, n):
                act.wait_ge(shifted, n)
                nc.scalar.activation(rexp[:, t0:t1, :], rb[:, t0:t1, :], ACT.Exp).then_inc(rexp_ready, 1)

            def copy_xnT(b):
                act.wait_ge(xnT_psum, b + 1)
                if b >= 1:
                    act.wait_ge(q_psum, b)
                nc.scalar.activation(xnT[:, :, :].rearrange("p c s -> p (c s)"), bank[0][:, :],
                                     ACT.Copy).then_inc(xnT_ready, 1)

            def exponentials(b, j):
                act.wait_ge(negmax_ready, TB * b + j + 1)
                if b >= 1:
                    act.wait_ge(pT_psum, 2 * b)
                for hh in range(KVH):
                    nc.scalar.activation(probs[:, j, hh, :], bank[2 + j][:, hh * A:(hh + 1) * A], ACT.Exp,
                                         bias=negmax[:, j, hh:hh + 1], scale=HD ** -0.5,
                                         accum_out=den[:, j, hh:hh + 1]).then_inc(exp_done, 1)

            copy_xnT(0)
            for t in range(B + 2):
                if t + 1 < B and t >= 1:
                    copy_xnT(t + 1)
                if t < B:
                    exponentials(t, 0)
                if t == B:
                    exp_logits(0, EARLY, 1)
                if 1 <= t <= B:
                    b = t - 1
                    act.wait_ge(o_psum, b + 1)
                    if b >= 1:
                        act.wait_ge(att_psum, b)
                    nc.scalar.activation(oT[:, :], bank[6][0:HD, 0:S], ACT.Copy).then_inc(oT_ready, 1)
                if t < B:
                    exponentials(t, 1)
                if t == 0:
                    copy_xnT(1)
                if t >= 2:
                    b = t - 2
                    act.wait_ge(xn2T_psum, b + 1)
                    if b >= 1:
                        act.wait_ge(lg_psum, b)
                    else:
                        act.wait_ge(zero_out, 16)
                        act.wait_ge(zero_xn2, 16)
                        act.wait_ge(zero_xe, 16)
                    nc.scalar.activation(xn2T[:, :, :].rearrange("p c s -> p (c s)"), bank[0][:, :],
                                         ACT.Copy).then_inc(xn2T_ready, 1)
                if t == 0:
                    act.wait_ge(v_psum, 1)
                    nc.scalar.activation(v[:, :], bank[7][0:A, :], ACT.Copy).then_inc(v_ready, 1)
                if t < B:
                    act.wait_ge(pT_psum, 2 * t + 1)
                    if t >= 1:
                        act.wait_ge(o_psum, t)
                    nc.scalar.activation(probsT[:, 0:2, :].rearrange("a h s -> a (h s)"), bank[4][0:A, :],
                                         ACT.Copy).then_inc(pT_copied, 1)
                    act.wait_ge(pT_psum, 2 * t + 2)
                    nc.scalar.activation(probsT[:, 2:4, :].rearrange("a h s -> a (h s)"), bank[5][0:A, :],
                                         ACT.Copy).then_inc(pT_copied, 1)
                if 1 <= t <= 4:
                    split_high(*divmod(t - 1, 3))
            split_high(1, 1)
            exp_logits(EARLY, NT, 2)
            split_high(1, 2)
            act.wait_ge(oh_block, 1)
            oh = oh_blocks.rearrange("p (k t s) -> p k t s", k=2, t=NT)
            t0 = CONSTS["token1"][0]
            for t in range(NT):
                nc.scalar.activation(marked[:, :, t, :], oh[:, :, t, :], ACT.Copy,
                                     scale=const[:, t0 + t:t0 + t + 1]).then_inc(marked_ready, 1)

            def stage(s):
                act.wait_ge(x_gathered, 16 * (s + 1))
                nc.scalar.activation(xs[:, :], xg_flat[:, bass.ds((s & (RING - 1)) * XW, D)],
                                     ACT.Copy).then_inc(x_staged, 1)
                nc.scalar.activation(weights[:, bass.ds((s & 7) * E, E)],
                                     xg_flat[:, bass.ds((s & (RING - 1)) * XW + D, E)], ACT.Copy)\
                  .then_inc(weights_kept, 1)

            def x_high(s, par):
                act.wait_ge(xT_made, s + 1)
                nc.scalar.activation(xT[:, par, 0, :, :].rearrange("p c t -> p (c t)"), bank[7][:, 0:D],
                                     ACT.Copy).then_inc(xT_hi, 1)

            def gate(s, hf):
                act.wait_ge(gu_made, 2 * s + hf + 1)
                if not isinstance(s, int) or s >= 1:
                    act.wait_ge(h_made, 2 * s + hf - 1)
                nc.scalar.activation(silu[:, hf, :], bank[2 * hf][:, :], ACT.Silu).then_inc(silu_made, 1)

            def h_high(s, hf):
                act.wait_ge(hT_made, 2 * s + hf + 1)
                nc.scalar.activation(hT[:, hf, 0, :], bank[4 + hf][:, :], ACT.Copy).then_inc(hT_hi, 1)

            def middle_piece(s):
                v = act.value_load(tab[0:1, 1, bass.ds(s, 1)], min_val=0, max_val=CODES)
                with act.If(v > 0):
                    split_high((v >> 3) + 1, 1)

            def end_pieces(s):
                v = act.value_load(tab[0:1, 2, bass.ds(s, 1)], min_val=0, max_val=CODES)
                with act.If(v > 0):
                    act.wait_ge(y_made, s)
                    for p in range(3):
                        with act.If((v & (1 << p)) > 0):
                            split_high((v >> 3) + 1, p)

            def step(s, par, first=False):
                gate(s, 0)
                if not first:
                    h_high(s - 1, 1)
                x_high(s + 1, 1 - par)
                stage(s + 2)
                if not first:
                    middle_piece(s)
                gate(s, 1)
                h_high(s, 0)
                if not first:
                    end_pieces(s)

            stage(0)
            x_high(0, 0)
            stage(1)
            step(0, 0, first=True)
            act.wait_ge(tables_ready, 1)
            with act.Fori(0, PAIRS) as i:
                step(i * 2 + 1, 1)
                step(i * 2 + 2, 0)

            def steps_while_used(i, u):
                s = i * 4 + (FULL - 1 + u)
                used = act.value_load(tab[0:1, 3, bass.ds(s, 1)], min_val=0, max_val=1)
                with act.If(used > 0):
                    step(s, (FULL - 1 + u) % 2)
                    if u < 3:
                        steps_while_used(i, u + 1)

            with act.Fori(0, (NBLK - FULL + 1) // 4) as i:
                steps_while_used(i, 0)
            last = act.value_load(last_block[0:1, 0:1], min_val=FULL - 1, max_val=NBLK - 1)
            h_high(last, 1)

        @block.tensor
        def _(pe):
            wka_v, wkb_v, wv_v, gw_v = (w.rearrange("p (c n) -> p c n", c=KC) for w in (wka, wkb, wv, gw))

            def project_keys(g):
                pe.wait_ge(ctx_in[g], 16)
                for n, w in enumerate((wka_v, wkb_v)):
                    for k in range(KC):
                        mm = nc.tensor.matmul(bank[2 + 2 * g + n][:, 0:4 * A], w[:, k, :],
                                              ctxT[:, k, 4 * A * g:4 * A * (g + 1)], start=(k == 0), stop=(k == KC - 1))
                mm.then_inc(k_psum, 1)

            def project_values(g):
                pe.wait_ge(ctx_in[g], 16)
                for b in range(4 * g, 4 * g + 4):
                    for k in range(KC):
                        mm = nc.tensor.matmul(bank[7][0:A, b * 64:(b + 1) * 64], ctxT[:, k, b * A:(b + 1) * A],
                                              wv_v[:, k, :], start=(k == 0), stop=(k == KC - 1))
                mm.then_inc(v_psum, 1)

            pe.wait_ge(wkv_in, 16)
            project_keys(0)
            pe.wait_ge(const_in, 16)

            def transpose_xn(b):
                pe.wait_ge(xn_ready, TB * (b + 1))
                if b >= 4:
                    pe.wait_ge(xn2T_ready, b - 3)
                for j in range(TB):
                    for k in range(KC):
                        mm = nc.tensor.transpose(bank[0][:, k * S + j * P:k * S + (j + 1) * P],
                                                 xn[:, b % 2, j, k * P:(k + 1) * P], ident)
                mm.then_inc(xnT_psum, 1)

            def project_q(b):
                pe.wait_ge(xnT_ready, b + 1)
                if b >= 1:
                    pe.wait_ge(qrot_ready, b)
                for k in range(KC):
                    mm = nc.tensor.matmul(bank[1][:, 0:S], raw_wq[:, k, 0, :], xnT[:, k, :],
                                          start=(k == 0), stop=(k == KC - 1))
                mm.then_inc(q_psum, 1)

            def stay_warm(n):
                for _ in range(n):
                    nc.tensor.matmul(bank[3][:, :], ident, const[:, 0:512], start=True, stop=True)

            transpose_xn(0)
            project_values(0)
            pe.wait_ge(wq_summed, 1)
            project_q(0)
            project_values(1)
            for t in range(B + 3):
                if t < B:
                    pe.wait_ge(qrot_ready, t + 1)
                    pe.wait_ge(kbd_ready, t + 1)
                    if t >= 1:
                        pe.wait_ge(exp_done, TB * KVH * t)
                    for j in range(TB):
                        nc.tensor.matmul(bank[2 + j][:, 0:KVH * A], qrot[:, j * P:(j + 1) * P],
                                         kbd[:, t % 2, :, :].rearrange("p h a -> p (h a)"),
                                         start=True, stop=True).then_inc(s_psum, 1)
                if t == 0:
                    project_keys(1)
                if t + 1 < B:
                    transpose_xn(t + 1)
                if t == B:
                    stay_warm(1)
                if 1 <= t <= B:
                    b = t - 1
                    pe.wait_ge(pT_copied, 2 * (b + 1))
                    pe.wait_ge(v_ready, 1)
                    if b >= 3:
                        pe.wait_ge(lg_ready, b - 2)
                    for hh in range(KVH):
                        mm = nc.tensor.matmul(bank[6][0:HD, 0:S], v[:, b * 64 + hh * HD:b * 64 + (hh + 1) * HD],
                                              probsT[:, hh, :], start=(hh == 0), stop=(hh == KVH - 1))
                    mm.then_inc(o_psum, 1)
                if t + 1 < B:
                    project_q(t + 1)
                if 1 <= t <= B:
                    b = t - 1
                    pe.wait_ge(oT_ready, b + 1)
                    if b == 0:
                        pe.wait_ge(wo_in, 16)
                    else:
                        pe.wait_ge(x2_ready, TB * b)
                    for j in range(TB):
                        mm = nc.tensor.matmul(bank[7][:, j * D:(j + 1) * D], oT[:, j * P:(j + 1) * P], wo[:, :],
                                              start=True, stop=True)
                    mm.then_inc(att_psum, 1)
                if t == B + 1:
                    stay_warm(1)
                if t >= 3:
                    b = t - 3
                    pe.wait_ge(xn2T_ready, b + 1)
                    if b >= 1:
                        pe.wait_ge(lg_ready, b)
                    for j in range(TB):
                        for k in range(KC):
                            mm = nc.tensor.matmul(bank[6][:, S + j * E:S + (j + 1) * E],
                                                  xn2T[:, k, j * P:(j + 1) * P], gw_v[:, k, :],
                                                  start=(k == 0), stop=(k == KC - 1))
                    mm.then_inc(lg_psum, 1)
                if 2 <= t < B + 2:
                    b = t - 2
                    pe.wait_ge(xn2_ready, TB * (b + 1))
                    if b >= 1:
                        pe.wait_ge(xn2T_ready, b)
                    for j in range(TB):
                        for k in range(KC):
                            mm = nc.tensor.transpose(bank[0][:, k * S + j * P:k * S + (j + 1) * P],
                                                     xn2[:, j, k * P:(k + 1) * P], ident)
                    mm.then_inc(xn2T_psum, 1)
                if t < B:
                    pe.wait_ge(probs_ready, TB * (t + 1))
                    if t == 0:
                        pe.wait_ge(krot_ready, 2)
                    else:
                        pe.wait_ge(pT_copied, 2 * t)
                    for g in range(2):
                        for hh in range(2):
                            for j in range(TB):
                                mm = nc.tensor.transpose(bank[4 + g][0:A, hh * S + j * P:hh * S + (j + 1) * P],
                                                         probs[:, j, 2 * g + hh, :], ident)
                        mm.then_inc(pT_psum, 1)

            stay_warm(3)
            pe.wait_ge(chosen_ready, 3)
            pe.wait_ge(pool_step, 1)
            flat = chosen[:, :, :].rearrange("p t e -> p (t e)")
            nc.tensor.matmul(bank[0][:, 0:(NT + 1) * E], before_bf[:, :], flat, start=True, stop=False)
            for t in range(NT):
                n = NT - t
                mm = nc.tensor.matmul(bank[0][:, (t + 1) * E:(NT + 1) * E], ones_bf[:, :],
                                      chosen[:, t:t + 1, :].broadcast_to([P, n, E]), start=False, stop=(t == NT - 1))
            mm.then_inc(rank_psum, 1)
            stay_warm(6)
            for m in range(2 * NT):
                t, k = m // 2, m % 2
                pe.wait_ge(marked_ready, t + 1)
                if t < NT - 4:
                    pe.wait_ge(onehot_ready, t // 4 + 1)
                    row = oh_dve[:, (t // 4 % 2) * 8 + k * 4 + t % 4, :]
                else:
                    pe.wait_ge(onehot_pool, m - (2 * NT - 8) + 1)
                    row = oh_pool[:, m - (2 * NT - 8), :]
                nc.tensor.matmul(bank[1][0:NCOL, 0:P], marked[:, k, t, :], row, start=(m == 0),
                                 stop=(m == 2 * NT - 1)).then_inc(onehot_used, 1)
            pe.wait_ge(slotT_ready, 1)
            nc.tensor.transpose(bank[2][:, 0:NCOL], slotT, ident[0:NCOL, 0:NCOL]).then_inc(slots_psum, 1)

            def transpose_x(s):
                pe.wait_ge(x_staged, s + 1)
                if not isinstance(s, int) or s >= 1:
                    pe.wait_ge(xT_split, s)
                for k in range(KC):
                    mm = nc.tensor.transpose(bank[7][:, k * P:(k + 1) * P], xs[:, k * P:(k + 1) * P], ident)
                mm.then_inc(xT_made, 1)

            def expand(s, par, hf, e):
                if hf == 0:
                    pe.wait_ge(xT_hi, s + 1)
                    pe.wait_ge(w_lo, (e + 1) * 3)
                if not isinstance(s, int) or s >= 1:
                    pe.wait_ge(h_made, 2 * s + hf - 1)
                where = e & 1
                for k in range(KC):
                    for xp, wp in ((0, 0), (0, 1), (1, 0)):
                        if hf == 0 and k == 0 and xp == 1:
                            pe.wait_ge(xT_split, s + 1)
                        for n, col in ((0, hf * HALF), (1, I + hf * HALF)):
                            mm = nc.tensor.matmul(bank[2 * hf + n][:, :], xT[:, par, xp, k, :],
                                                  gu_part(where, wp, k * 2 * I + col, HALF),
                                                  start=(k == 0 and xp == 0 and wp == 0), stop=(k == KC - 1 and xp == 1))
                mm.then_inc(gu_made, 1)

            def transpose_h(s, hf):
                pe.wait_ge(h_made, 2 * s + hf + 1)
                if not isinstance(s, int) or s >= 1:
                    pe.wait_ge(hT_split, 2 * s + hf - 1)
                for j in range(JH):
                    mm = nc.tensor.transpose(bank[4 + hf][:, j * P:(j + 1) * P], h[:, hf, j * P:(j + 1) * P], ident)
                mm.then_inc(hT_made, 1)

            def contract(s, hf, e):
                pe.wait_ge(hT_split, 2 * s + hf + 1)
                if hf == 0 and (not isinstance(s, int) or s >= 1):
                    pe.wait_ge(y_out, s)
                where = e & 1
                for j in range(JH):
                    for hp, wp in ((0, 0), (0, 1), (1, 0)):
                        mm = nc.tensor.matmul(bank[6][:, 0:D], hT[:, hf, hp, j * P:(j + 1) * P],
                                              dn_part(where, wp, (hf * JH + j) * D, D),
                                              start=(hf == 0 and j == 0 and hp == 0 and wp == 0),
                                              stop=(hf == 1 and j == JH - 1 and hp == 1))
                if hf == 1:
                    mm.then_inc(y_made, 1)

            def expert_of(s):
                return pe.value_load(tab[0:1, 0, bass.ds(s, 1)], min_val=0, max_val=E - 1)

            def step(s, par, first=False):
                e = expert_of(s)
                expand(s, par, 0, e)
                if not first:
                    e_before = expert_of(s - 1)
                    transpose_h(s - 1, 1)
                    contract(s - 1, 0, e_before)
                transpose_x(s + 1)
                expand(s, par, 1, e)
                transpose_h(s, 0)
                if not first:
                    contract(s - 1, 1, e_before)

            stay_warm(5)
            pe.wait_ge(idx_ready, 1)
            transpose_x(0)
            pe.wait_ge(experts_ready, 1)
            step(0, 0, first=True)
            pe.wait_ge(tables_ready, 1)
            with pe.Fori(0, PAIRS) as i:
                step(i * 2 + 1, 1)
                step(i * 2 + 2, 0)

            def steps_while_used(i, u):
                s = i * 4 + (FULL - 1 + u)
                used = pe.value_load(tab[0:1, 3, bass.ds(s, 1)], min_val=0, max_val=1)
                with pe.If(used > 0):
                    step(s, (FULL - 1 + u) % 2)
                    if u < 3:
                        steps_while_used(i, u + 1)

            with pe.Fori(0, (NBLK - FULL + 1) // 4) as i:
                steps_while_used(i, 0)
            last = pe.value_load(last_block[0:1, 0:1], min_val=FULL - 1, max_val=NBLK - 1)
            e_last = expert_of(last)
            transpose_h(last, 1)
            contract(last, 0, e_last)
            contract(last, 1, e_last)

        @block.vector
        def _(dve):
            V = nc.vector
            n_step = [0]

            def link(ins):
                n_step[0] += 1
                ins.then_inc(dve_step, 1)
                dve.wait_ge(dve_step, n_step[0])

            def moments(b, into, sig):
                for t in range(TB * b, TB * b + TB):
                    V.bn_stats(stats[:, t, :], x[:, t, :]).then_inc(dve_step, 1)
                    n_step[0] += 1
                for t in range(TB * b, TB * b + TB):
                    dve.wait_ge(dve_step, n_step[0] - TB + 1 + t - TB * b)
                    V.bn_aggr(into[:, t, :], stats[:, t, :]).then_inc(sig, 1)

            def settle():
                dve.wait_ge(dve_step, n_step[0])

            def normalise(b):
                dve.wait_ge(rstd_ready, b + 1)
                dve.wait_ge(moments1, TB * (b + 1))
                if b >= 2:
                    dve.wait_ge(xnT_psum, b - 1)
                for j in range(TB):
                    t = TB * b + j
                    V.tensor_scalar(xn[:, b % 2, j, :], x[:, t, :], mv[:, t, 0:1], rstd[:, t:t + 1],
                                    ALU.subtract, ALU.mult).then_inc(xn_ready, 1)

            def per_tile(ap):
                return ap.rearrange("p (t o) -> p t o", o=1).broadcast_to([P, ap.shape[-1], E])

            def per_expert(ap, n=NT):
                return ap.rearrange("p (o e) -> p o e", o=1).broadcast_to([P, n, E])

            def largest(k, t0, t1, src):
                link(V.tensor_reduce(pmax[:, k, t0:t1], src[:, t0:t1, :], AX.X, ALU.max))
                link(V.tensor_tensor(rb[:, t0:t1, :], src[:, t0:t1, :], per_tile(pmax[:, k, t0:t1]), ALU.is_equal))
                link(V.tensor_tensor(rb[:, t0:t1, :], rb[:, t0:t1, :], per_expert(c("prio"), t1 - t0), ALU.mult))
                link(V.tensor_reduce(pscore[:, t0:t1], rb[:, t0:t1, :], AX.X, ALU.max))
                link(V.tensor_tensor(pick[:, k, t0:t1, :], rb[:, t0:t1, :], per_tile(pscore[:, t0:t1]), ALU.is_equal))

            def choose_first(t0, t1, n):
                link(V.tensor_reduce(pscore[:, t0:t1], logits[:, t0:t1, :], AX.X, ALU.max))
                V.tensor_tensor(rb[:, t0:t1, :], logits[:, t0:t1, :], per_tile(pscore[:, t0:t1]),
                                ALU.subtract).then_inc(shifted, 1)
                dve.wait_ge(rexp_ready, n)
                largest(0, t0, t1, rexp)

            def choose_second(t0, t1):
                link(V.scalar_tensor_tensor(out=ra[:, t0:t1, :], in0=pick[:, 0, t0:t1, :], scalar=-4.0,
                                            in1=rexp[:, t0:t1, :], op0=ALU.mult, op1=ALU.add))
                largest(1, t0, t1, ra)
                V.tensor_tensor(chosen[:, t0:t1, :], pick[:, 0, t0:t1, :], pick[:, 1, t0:t1, :],
                                ALU.add).then_inc(chosen_ready, 1)

            EARLY = TB * (B - 3)
            dve.wait_ge(x_in[0], 16)
            moments(0, mv, moments1)

            def rope_keys(g):
                dve.wait_ge(k_psum, g + 1)
                kr = krot[:, 4 * g:4 * g + 4, :]
                both = lambda n: c(n).rearrange("p (o a) -> p o a", o=1).broadcast_to([P, 4, A])
                V.tensor_tensor(kr, bank[2 + 2 * g][:, 0:4 * A].rearrange("p (b a) -> p b a", b=4), both("kcos"),
                                ALU.mult).then_inc(dve_step, 1)
                V.tensor_tensor(ktmp, bank[3 + 2 * g][:, 0:4 * A].rearrange("p (b a) -> p b a", b=4),
                                both("ksin"), ALU.mult).then_inc(dve_step, 1)
                n_step[0] += 2
                settle()
                V.tensor_tensor(kr, kr, ktmp, ALU.add).then_inc(krot_ready, 1)

            normalise(0)
            dve.wait_ge(wq_in, 16)
            link(V.tensor_tensor(wq, wq, raw_wq[:, :, 1, :], ALU.add))
            link(V.tensor_tensor(wq, wq, raw_wq[:, :, 2, :], ALU.add))
            V.tensor_tensor(wq, wq, raw_wq[:, :, 3, :], ALU.add).then_inc(wq_summed, 1)
            dve.wait_ge(const_in, 16)
            rope_keys(0)
            def normalise2(b):
                dve.wait_ge(rstd2_ready, b + 1)
                dve.wait_ge(moments2, TB * (b + 1))
                if b >= 1:
                    dve.wait_ge(xn2T_psum, b)
                    dve.wait_ge(xn2_out, 16 * b)
                for j in range(TB):
                    t = TB * b + j
                    V.tensor_scalar(xn2[:, j, :], x[:, t, :], mv2[:, t, 0:1], rstd2[:, t:t + 1],
                                    ALU.subtract, ALU.mult).then_inc(xn2_ready, 1)

            def rotate_q(b):
                dve.wait_ge(q_psum, b + 1)
                if b >= 1:
                    dve.wait_ge(s_psum, TB * b)
                V.tensor_tensor(qrot[:, :], bank[1][:, 0:S], c("rope"), ALU.mult).then_inc(qrot_ready, 1)

            def normalise_probs(b, j):
                dve.wait_ge(exp_done, KVH * (TB * b + j + 1))
                link(V.reciprocal(den[:, j, :], den[:, j, :]))
                V.tensor_tensor(probs[:, j, :, :], probs[:, j, :, :],
                                den[:, j, :].rearrange("p (h o) -> p h o", o=1).broadcast_to([P, KVH, A]),
                                ALU.mult).then_inc(probs_ready, 1)

            rotate_q(0)
            dve.wait_ge(x_in[1], 16)
            moments(1, mv, moments1)
            for t in range(B + 3):
                if t < B:
                    for j in range(TB):
                        dve.wait_ge(s_psum, TB * t + j + 1)
                        link(V.tensor_reduce(negmax[:, j, :],
                                             bank[2 + j][:, 0:KVH * A].rearrange("p (h a) -> p h a", h=KVH),
                                             AX.X, ALU.max))
                        V.tensor_scalar(negmax[:, j, :], negmax[:, j, :], -(HD ** -0.5), None,
                                        ALU.mult).then_inc(negmax_ready, 1)
                if t == 0:
                    normalise(1)
                    dve.wait_ge(x_in[2], 16)
                    moments(2, mv, moments1)
                    normalise_probs(0, 0)
                    normalise_probs(0, 1)
                    dve.wait_ge(krot_ready, 1)
                    rope_keys(1)
                if 2 <= t < B + 2:
                    normalise2(t - 2)
                if t == B:
                    dve.wait_ge(lg_ready, B - 3)
                    choose_first(0, EARLY, 1)
                if t == B + 1:
                    choose_second(0, EARLY)
                if t + 2 < B:
                    normalise(t + 2)
                if t + 1 < B:
                    rotate_q(t + 1)
                if 1 <= t < B:
                    normalise_probs(t, 0)
                    normalise_probs(t, 1)
                if 1 <= t <= B:
                    b = t - 1
                    dve.wait_ge(att_psum, b + 1)
                    for j in range(TB):
                        tt = TB * b + j
                        V.scalar_tensor_tensor(out=x[:, tt, :], in0=bank[7][:, j * D:(j + 1) * D], scalar=tg[:, 0:1],
                                               in1=x[:, tt, :], op0=ALU.mult, op1=ALU.add).then_inc(x2_ready, 1)
                if 1 <= t <= B:
                    dve.wait_ge(x2_ready, TB * t)
                    moments(t - 1, mv2, moments2)
                if t + 3 < B:
                    dve.wait_ge(x_in[t + 3], 16)
                    moments(t + 3, mv, moments1)
                if t == 0:
                    dve.wait_ge(masks_in, 16)
                    link(V.tensor_copy(before_bf[:, :], c("before")))
                    V.memset(chosen[:, NT:NT + 1, :], 0.0).then_inc(chosen_ready, 1)
                    dve.wait_ge(tanh_ready, 1)
                    link(V.tensor_scalar(tg[:, 0:1], tg[:, 0:1], 1.0 / KVH, None, ALU.mult))
                if t >= 3:
                    b = t - 3
                    dve.wait_ge(lg_psum, b + 1)
                    V.tensor_copy(logits[:, TB * b:TB * b + TB, :].rearrange("p t e -> p (t e)"),
                                  bank[6][:, S:S + TB * E]).then_inc(lg_ready, 1)

            dve.wait_ge(lg_ready, B)
            choose_first(EARLY, NT, 2)
            choose_second(EARLY, NT)
            link(V.tensor_tensor(pscore[:, :], pmax[:, 0, :], pmax[:, 1, :], ALU.add))
            link(V.reciprocal(pscore[:, :], pscore[:, :]))
            link(V.tensor_scalar(pscore[:, :], pscore[:, :], tg[:, 1:2], None, ALU.mult))
            dve.wait_ge(chosen_ready, 3)
            link(V.tensor_tensor(wdense[:, :, :], rexp[:, :, :], chosen[:, 0:NT, :], ALU.mult))
            V.tensor_tensor(wdense[:, :, :], wdense[:, :, :], per_tile(pscore[:, :]), ALU.mult).then_inc(wdense_ready, 1)
            dve.wait_ge(rank_psum, 1)
            NS = T // P
            cmp_ = count_area[:, 0:E * NS].rearrange("p (e n) -> p e n", e=E)
            link(V.tensor_tensor(cmp_, bank[0][:, NT * E:(NT + 1) * E].rearrange("p (e o) -> p e o", o=1)
                                 .broadcast_to([P, E, NS]),
                                 c("steps").rearrange("p (o n) -> p o n", o=1).broadcast_to([P, E, NS]), ALU.is_gt))
            link(V.tensor_reduce(nblk[:, :], cmp_, AX.X, ALU.add))
            cum = count_area[:, 0:E * E].rearrange("p (e n) -> p e n", e=E)
            link(V.tensor_tensor(cum, c("earlier").rearrange("p (e n) -> p e n", e=E),
                                 nblk[:, :].rearrange("p (o e) -> p o e", o=1).broadcast_to([P, E, E]), ALU.mult))
            link(V.tensor_reduce(startblk[:, :], cum, AX.X, ALU.add))
            link(V.scalar_tensor_tensor(out=slotpos[:, :, :], in0=per_expert(startblk[:, :]), scalar=float(P),
                                        in1=bank[0][:, 0:NT * E].rearrange("p (t e) -> p t e", e=E),
                                        op0=ALU.mult, op1=ALU.add))
            link(V.tensor_tensor(prod, pick, slotpos[:, :, :].rearrange("p (o t) e -> p o t e", o=1)
                                 .broadcast_to([P, 2, NT, E]), ALU.mult))
            link(V.tensor_reduce(rank[:, :], prod.rearrange("p k t e -> p (k t) e"), AX.X, ALU.add))
            link(V.tensor_copy(rank_i[:, 0, :], rank[:, :]))
            V.tensor_scalar(rank_i[:, 1, :], rank_i[:, 0, :], P - 1, None, ALU.bitwise_and).then_inc(dve_step, 1)
            n_step[0] += 1
            link(V.tensor_scalar(rank_i[:, 0, :], rank_i[:, 0, :], 7, None, ALU.arith_shift_right))
            V.tensor_copy(slot_f[:, 1, :], rank_i[:, 1, :]).then_inc(row_ready, 1)
            link(V.tensor_copy(slot_f[:, 0, :], rank_i[:, 0, :]))
            V.tensor_tensor(oh_blocks.rearrange("p (n s) -> p n s", n=2 * NT),
                            slot_f[:, 0, :].rearrange("p (n o) -> p n o", o=1).broadcast_to([P, 2 * NT, NCOL]),
                            c("blocks").rearrange("p (o s) -> p o s", o=1).broadcast_to([P, 2 * NT, NCOL]),
                            ALU.is_equal).then_inc(oh_block, 1)
            dve.wait_ge(row_ready, 1)
            rows_of = slot_f[:, 1, :].rearrange("p (k t) -> p k t", k=2)
            for g in range((NT - 4) // 4):
                if g >= 2:
                    dve.wait_ge(onehot_used, 8 * (g - 1))
                V.tensor_tensor(oh_dve[:, 8 * (g % 2):8 * (g % 2) + 8, :].rearrange("p (k t) q -> p k t q", k=2),
                                c("iota").rearrange("p (o r q) -> p o r q", o=1, r=1).broadcast_to([P, 2, 4, P]),
                                rows_of[:, :, 4 * g:4 * g + 4].rearrange("p k (t o) -> p k t o", o=1)
                                .broadcast_to([P, 2, 4, P]), ALU.is_equal).then_inc(onehot_ready, 1)
            all_blocks = c("blocks").rearrange("p (s o) -> p s o", o=1).broadcast_to([P, NCOL, E])
            for_blocks = lambda ap: ap.rearrange("p (o e) -> p o e", o=1).broadcast_to([P, NCOL, E])
            link(V.tensor_tensor(endblk[:, :], startblk[:, :], nblk[:, :], ALU.add))
            link(V.tensor_tensor(by_block, for_blocks(endblk[:, :]), all_blocks, ALU.is_le))
            link(V.tensor_reduce(tabf[:, 0, :], by_block, AX.X, ALU.add))
            V.tensor_scalar(tab[:, 0, :], tabf[:, 0, :], float(E - 1), None, ALU.min).then_inc(experts_ready, 1)
            dve.wait_ge(onehot_used, 2 * NT)
            V.tensor_copy(slotT, bank[1][0:NCOL, 0:P]).then_inc(slotT_ready, 1)
            dve.wait_ge(slots_psum, 1)
            link(V.tensor_scalar(empty, bank[2][:, 0:NCOL], 0.0, c("spare"), ALU.is_equal, ALU.mult))
            V.scalar_tensor_tensor(out=idx[:, :], in0=empty, scalar=-1.0, in1=bank[2][:, 0:NCOL],
                                   op0=ALU.add, op1=ALU.add).then_inc(idx_ready, 1)
            link(V.tensor_scalar(last_block[:, :], endblk[:, E - 1:E], -1.0, None, ALU.add))
            link(V.tensor_scalar(tab[:, 3, :], c("blocks"), endblk[:, E - 1:E], None, ALU.is_lt))
            link(V.tensor_copy(piece_at[:, 0, :], startblk[:, :]))
            link(V.tensor_scalar(piece_at[:, 1, :], nblk[:, :], 1.0, -float(NCOL), ALU.is_equal, ALU.mult))
            link(V.scalar_tensor_tensor(out=piece_at[:, 1, :], in0=piece_at[:, 1, :], scalar=1.0,
                                        in1=startblk[:, :], op0=ALU.add, op1=ALU.add))
            link(V.scalar_tensor_tensor(out=piece_code[:, 0, :], in0=nblk[:, :], scalar=1.0, in1=c("alone"),
                                        op0=ALU.is_equal, op1=ALU.mult))
            link(V.tensor_tensor(piece_code[:, 0, :], piece_code[:, 0, :], c("first"), ALU.add))
            link(V.tensor_copy(piece_code[:, 1, :], c("second")))
            for n in range(2):
                link(V.tensor_tensor(by_piece[:, n, :, :], for_blocks(piece_at[:, n, :]), all_blocks, ALU.is_equal))
                link(V.tensor_tensor(by_piece[:, n, :, :], by_piece[:, n, :, :], for_blocks(piece_code[:, n, :]),
                                     ALU.mult))
            link(V.tensor_reduce(tabf[:, 1:3, :].rearrange("p n s -> p (n s)"),
                                 by_piece.rearrange("p n s e -> p (n s) e"), AX.X, ALU.add))
            link(V.tensor_copy(tab[:, 1, :], tabf[:, 2, :]))
            V.tensor_tensor(tab[:, 2, :], tabf[:, 1, :], tabf[:, 2, :], ALU.add).then_inc(tables_ready, 1)

            def x_low(s, par):
                dve.wait_ge(xT_hi, s + 1)
                V.tensor_tensor(xT[:, par, 1, :, :].rearrange("p c t -> p (c t)"), bank[7][:, 0:D],
                                xT[:, par, 0, :, :].rearrange("p c t -> p (c t)"), ALU.subtract).then_inc(xT_split, 1)

            def product(s, hf):
                dve.wait_ge(silu_made, 2 * s + hf + 1)
                if not isinstance(s, int) or s >= 1:
                    dve.wait_ge(hT_made, 2 * s + hf - 1)
                V.tensor_tensor(h[:, hf, :], silu[:, hf, :], bank[2 * hf + 1][:, :], ALU.mult).then_inc(h_made, 1)

            def h_low(s, hf):
                dve.wait_ge(hT_hi, 2 * s + hf + 1)
                V.tensor_tensor(hT[:, hf, 1, :], bank[4 + hf][:, :], hT[:, hf, 0, :], ALU.subtract)\
                 .then_inc(hT_split, 1)

            def weigh(s, last=False):
                e = dve.value_load(tab[0:1, 0, bass.ds(s, 1)], min_val=0, max_val=E - 1)
                dve.wait_ge(weights_kept, s + 1)
                dve.wait_ge(y_made, s + 1)
                if last:
                    dve.wait_ge(y_free, s + RING)
                else:
                    dve.wait_ge(y_free, s + 1)
                out = y[:, 0, :] if last else y[:, :, :].rearrange("p r d -> p (r d)")[:, bass.ds((s & (RING - 1)) * D, D)]
                V.tensor_scalar(out, bank[6][:, 0:D], weights[:, bass.ds((s & 7) * E + e, 1)],
                                None, ALU.mult).then_inc(y_out, 1)

            def step(s, par, first=False):
                product(s, 0)
                if not first:
                    h_low(s - 1, 1)
                x_low(s + 1, 1 - par)
                product(s, 1)
                h_low(s, 0)
                if not first:
                    weigh(s - 1)

            x_low(0, 0)
            step(0, 0, first=True)
            with dve.Fori(0, PAIRS) as i:
                step(i * 2 + 1, 1)
                step(i * 2 + 2, 0)

            def steps_while_used(i, u):
                s = i * 4 + (FULL - 1 + u)
                used = dve.value_load(tab[0:1, 3, bass.ds(s, 1)], min_val=0, max_val=1)
                with dve.If(used > 0):
                    step(s, (FULL - 1 + u) % 2)
                    if u < 3:
                        steps_while_used(i, u + 1)

            with dve.Fori(0, (NBLK - FULL + 1) // 4) as i:
                steps_while_used(i, 0)
            last = dve.value_load(last_block[0:1, 0:1], min_val=FULL - 1, max_val=NBLK - 1)
            h_low(last, 1)
            weigh(last, last=True)


def shape_constants():
    out = np.zeros((P, NCONST), np.float32)

    def put(name, value):
        a, b = CONSTS[name]
        out[:, a:b] = value

    inv = (np.float32(1.0) / np.float32(10000.0) ** (np.arange(0, HD, 2, dtype=np.float32) / np.float32(HD)))
    ang = np.arange(S, dtype=np.float32)[:, None] * inv[None, :].astype(np.float32)
    cos, sin = np.cos(ang).astype(np.float32), np.sin(ang).astype(np.float32)
    row = np.arange(P) % HR
    d = row % HD
    sign = np.where(d % 2 == 0, -1.0, 1.0).astype(np.float32)[:, None]
    put("ident", np.eye(P))
    put("rope", np.where((row < HD)[:, None], cos[:, d // 2].T, sign * sin[:, d // 2].T))
    put("kcos", cos[:A, d // 2].T)
    put("ksin", sign * sin[:A, d // 2].T)
    put("headmask", np.repeat((np.arange(P)[:, None] // HR == np.arange(KVH)[None, :]), A, axis=1))
    put("before", np.arange(P)[:, None] < np.arange(P)[None, :])
    put("iota", np.arange(P)[None, :])
    put("prio", E - np.arange(E)[None, :])
    put("steps", np.where(np.arange(T // P) == 0, -1, P * np.arange(T // P))[None, :])
    put("earlier", (np.arange(E)[None, :] < np.arange(E)[:, None]).reshape(1, E * E))
    put("blocks", np.arange(NCOL)[None, :])
    put("token1", np.arange(NT)[None, :] * P + np.arange(P)[:, None] + 1)
    e = np.arange(E)
    leads = (e >= 1) & (e <= E - 2)
    put("first", np.where(leads, 8 * e + 1, 0)[None, :])
    put("alone", np.where(leads, 6, 0)[None, :])
    put("second", np.where(leads, 8 * e + 4, 0)[None, :])
    put("spare", np.arange(P)[:, None] + T + 1)
    return out


def kernel(**inputs):
    import concourse.bacc as bacc
    from concourse.bass_utils import run_bass_kernel_spmd

    x = np.ascontiguousarray(inputs["x"]).reshape(T, D)
    ctx = np.ascontiguousarray(inputs["ctx_1024"])
    Wq, Wk, Wv, Wo = (np.ascontiguousarray(inputs[f"L0_xattn_{n}"]) for n in ("Wq", "Wk", "Wv", "Wo"))
    gate = np.ascontiguousarray(inputs["L0_ffn_gate_w"])
    gup = np.ascontiguousarray(inputs["L0_ffn_gate_up_proj"])
    down = np.ascontiguousarray(inputs["L0_ffn_down_proj"])
    g2 = np.concatenate([np.ascontiguousarray(inputs["g_xattn"]), np.ascontiguousarray(inputs["g_ffn"])])

    swap = np.arange(HD) ^ 1

    def by_chunk(a):
        return a.reshape(KC, P, -1).transpose(1, 0, 2).reshape(P, -1)

    q4 = Wq.reshape(D, KVH, GROUPS, HD).transpose(0, 2, 1, 3)
    q4 = np.concatenate([q4, q4[..., swap]], axis=-1).reshape(D, -1)
    ka = np.concatenate([Wk, Wk], axis=-1).reshape(D, -1)
    kb = np.concatenate([Wk[..., swap], Wk[..., swap]], axis=-1).reshape(D, -1)
    small = np.concatenate([by_chunk(ka), by_chunk(kb), by_chunk(Wv.reshape(D, -1)),
                            by_chunk(gate.T), np.broadcast_to(g2[None, :], (P, 2)), by_chunk(q4)], axis=1)
    arrays = {
        "x": x,
        "ctxT": ctx.reshape(B * A, KC, P).transpose(2, 1, 0),
        "small": small,
        "wo": Wo,
        "gu": gup.transpose(0, 2, 1).reshape(E, KC, P, 2 * I).transpose(0, 2, 1, 3).reshape(E, P, GU),
        "dn": down.transpose(0, 2, 1).reshape(E, I // P, P, D).transpose(0, 2, 1, 3).reshape(E, P, DN),
        "consts": shape_constants(),
    }
    arrays = {k: np.ascontiguousarray(a) for k, a in arrays.items()}
    nc = bacc.Bacc("TRN2", target_bir_lowering=False, num_devices=1)
    aps = [nc.dram_tensor(f"in_{k}", a.shape, mybir.dt.from_np(a.dtype), kind="ExternalInput").ap() for k, a in arrays.items()]
    out = nc.dram_tensor("out", (T + P, D), F32, kind="ExternalOutput").ap()
    build_program(nc, *aps, out)
    r = run_bass_kernel_spmd(nc, [{f"in_{k}": a for k, a in arrays.items()}], core_ids=[0])
    return r.results[0]["out"][:T].reshape(B, S, D)
```
